# Optimizing a Trainium2 kernel written in Bass

```python
import numpy as np
import jax
import jax.numpy as jnp

def _softmax(x, axis=-1):
    return jax.nn.softmax(x, axis=axis)

def _gelu(x):
    return jax.nn.gelu(x, approximate=True)

def _silu(x):
    return jax.nn.silu(x)

def _sigmoid(x):
    return jax.nn.sigmoid(x)

def _layernorm(x, axis=-1, eps=1e-05):
    m = jnp.mean(x, axis=axis, keepdims=True)
    v = jnp.var(x, axis=axis, keepdims=True)
    return (x - m) / jnp.sqrt(v + eps)

def _scatter_add(tgt, idx, src, axis=0):
    return tgt.at[idx].add(src)

def _segment_sum(src, seg, n):
    return jax.ops.segment_sum(src, seg, n)
kernel_name = 'mk_sandwich_d1_jaxref_r4_552781'

def setup_inputs(seed: int=0):
    np.random.seed(seed)
    _w = jnp.asarray

    def _L0_attn_setup():
        import jax, jax.numpy as jnp
        import numpy as np
        B, S, D, M, TOPK = (4, 512, 256, 4, 2)

        def _linear_scan(x_scan, a):

            def combine(c1, c2):
                a1, x1 = c1
                a2, x2 = c2
                return (a1 * a2, a2 * x1 + x2)
            _, h = jax.lax.associative_scan(combine, (a, x_scan), axis=-2)
            return h
        key = jax.random.key(seed)
        ks = jax.random.split(key, 8)
        s = 1.0 / np.sqrt(D)
        return {'x': jax.random.normal(ks[0], (B, S, D), jnp.float32), 'Wg': jax.random.uniform(ks[1], (M, D, D), jnp.float32, -s, s), 'bg': jax.random.uniform(ks[2], (M, D), jnp.float32, -s, s), 'Wv': jax.random.uniform(ks[3], (M, D, D), jnp.float32, -s, s), 'bv': jax.random.uniform(ks[4], (M, D), jnp.float32, -s, s), 'Wd': jax.random.uniform(ks[5], (M, D, D), jnp.float32, -s, s), 'bd': jnp.ones((M, D), jnp.float32), 'gate_W': jax.random.uniform(ks[6], (D, M), jnp.float32, -s, s)}
    _L0_attn_in = _L0_attn_setup()

    def _L0_ffn_setup():
        import jax, jax.numpy as jnp
        import numpy as np
        B, S, D, H, E = (64, 256, 256, 64, 8)
        EPS = 1e-05
        key = jax.random.key(seed)
        ks = jax.random.split(key, 8)
        x = jax.random.normal(ks[0], (B, S, D), jnp.float32)
        return {'x': x, 'ln_g': jnp.ones((D,), jnp.float32), 'ln_b': jnp.zeros((D,), jnp.float32), 'bn_g': jnp.ones((D,), jnp.float32), 'bn_b': jnp.zeros((D,), jnp.float32), 'bn_mean': jax.random.normal(ks[1], (D,), jnp.float32) * 0.01, 'bn_var': jnp.ones((D,), jnp.float32), 'Wr': jax.random.normal(ks[2], (D, E), jnp.float32) * 0.02, 'br': jnp.zeros((E,), jnp.float32), 'W_down': jax.random.normal(ks[3], (E, D, H), jnp.float32) * 0.02, 'b_down': jnp.zeros((E, H), jnp.float32), 'W_up': jax.random.normal(ks[4], (E, H, D), jnp.float32) * 0.02, 'b_up': jnp.zeros((E, D), jnp.float32)}
    _L0_ffn_in = _L0_ffn_setup()
    _d = {'L0_attn_x': _L0_attn_in['x'], 'L0_attn_Wg': _L0_attn_in['Wg'], 'L0_attn_bg': _L0_attn_in['bg'], 'L0_attn_Wv': _L0_attn_in['Wv'], 'L0_attn_bv': _L0_attn_in['bv'], 'L0_attn_Wd': _L0_attn_in['Wd'], 'L0_attn_bd': _L0_attn_in['bd'], 'L0_attn_gate_W': _L0_attn_in['gate_W'], 'L0_ffn_ln_g': _L0_ffn_in['ln_g'], 'L0_ffn_ln_b': _L0_ffn_in['ln_b'], 'L0_ffn_bn_g': _L0_ffn_in['bn_g'], 'L0_ffn_bn_b': _L0_ffn_in['bn_b'], 'L0_ffn_bn_mean': _L0_ffn_in['bn_mean'], 'L0_ffn_bn_var': _L0_ffn_in['bn_var'], 'L0_ffn_Wr': _L0_ffn_in['Wr'], 'L0_ffn_br': _L0_ffn_in['br'], 'L0_ffn_W_down': _L0_ffn_in['W_down'], 'L0_ffn_b_down': _L0_ffn_in['b_down'], 'L0_ffn_W_up': _L0_ffn_in['W_up'], 'L0_ffn_b_up': _L0_ffn_in['b_up']}
    _x0 = _d['L0_attn_x']
    _d['L0_attn_x'] = jax.random.normal(jax.random.fold_in(jax.random.key(seed), 1), (8, 1024, 256), dtype=_x0.dtype)
    del _x0
    return _d

def reference(L0_attn_x, L0_attn_Wg, L0_attn_bg, L0_attn_Wv, L0_attn_bv, L0_attn_Wd, L0_attn_bd, L0_attn_gate_W, L0_ffn_ln_g, L0_ffn_ln_b, L0_ffn_bn_g, L0_ffn_bn_b, L0_ffn_bn_mean, L0_ffn_bn_var, L0_ffn_Wr, L0_ffn_br, L0_ffn_W_down, L0_ffn_b_down, L0_ffn_W_up, L0_ffn_b_up):

    def _L0_attn_ref(x, Wg, bg, Wv, bv, Wd, bd, gate_W):
        import jax, jax.numpy as jnp
        import numpy as np
        B, S, D, M, TOPK = (4, 512, 256, 4, 2)

        def _linear_scan(x_scan, a):

            def combine(c1, c2):
                a1, x1 = c1
                a2, x2 = c2
                return (a1 * a2, a2 * x1 + x2)
            _, h = jax.lax.associative_scan(combine, (a, x_scan), axis=-2)
            return h
        gate_logits = jnp.einsum('bsd,dm->bsm', x, gate_W)
        top_vals, top_idx = jax.lax.top_k(gate_logits, TOPK)
        weights = jax.nn.softmax(top_vals, axis=-1)
        g = jnp.einsum('bsd,mde->mbse', x, Wg) + bg[:, None, None, :]
        v = jnp.einsum('bsd,mde->mbse', x, Wv) + bv[:, None, None, :]
        d = jnp.einsum('bsd,mde->mbse', x, Wd) + bd[:, None, None, :]
        x_scan = jax.nn.sigmoid(g) * jnp.tanh(v)
        a = 0.001 + 0.998 * jax.nn.sigmoid(d)
        h = _linear_scan(x_scan, a)
        comb = jnp.sum(jax.nn.one_hot(top_idx, M, dtype=x.dtype) * weights[..., None], axis=-2)
        return jnp.einsum('bsm,mbsd->bsd', comb, h)

    def _L0_ffn_ref(x, ln_g, ln_b, bn_g, bn_b, bn_mean, bn_var, Wr, br, W_down, b_down, W_up, b_up):
        import jax, jax.numpy as jnp
        import numpy as np
        B, S, D, H, E = (64, 256, 256, 64, 8)
        EPS = 1e-05
        mu = jnp.mean(x, axis=-1, keepdims=True)
        var = jnp.var(x, axis=-1, keepdims=True)
        z = (x - mu) * jax.lax.rsqrt(var + EPS) * ln_g + ln_b
        z_sent = jnp.mean(z, axis=1)
        z_bn = (z_sent - bn_mean) * jax.lax.rsqrt(bn_var + EPS) * bn_g + bn_b
        probs = jax.nn.softmax(z_bn @ Wr + br, axis=-1)
        idx = jnp.argmax(probs, axis=-1)
        gate = jnp.take_along_axis(probs, idx[:, None], axis=1)[:, 0]
        h = jax.nn.relu(jnp.einsum('bsd,bdh->bsh', z, W_down[idx]) + b_down[idx][:, None, :])
        y = jnp.einsum('bsh,bhd->bsd', h, W_up[idx]) + b_up[idx][:, None, :]
        return y * gate[:, None, None]
    x = L0_attn_x
    x = x + _layernorm(_L0_attn_ref(_layernorm(x, axis=-1), L0_attn_Wg, L0_attn_bg, L0_attn_Wv, L0_attn_bv, L0_attn_Wd, L0_attn_bd, L0_attn_gate_W), axis=-1)
    x = x + _layernorm(_L0_ffn_ref(_layernorm(x, axis=-1), L0_ffn_ln_g, L0_ffn_ln_b, L0_ffn_bn_g, L0_ffn_bn_b, L0_ffn_bn_mean, L0_ffn_bn_var, L0_ffn_Wr, L0_ffn_br, L0_ffn_W_down, L0_ffn_b_down, L0_ffn_W_up, L0_ffn_b_up), axis=-1)
    return x

_drawn_inputs = setup_inputs


def setup_inputs(seed=0):
    import zlib

    import numpy as np

    out = dict(_drawn_inputs(seed))
    spreads = {'L0_attn_bd': (1.0, 0.2),
     'L0_ffn_ln_g': (1.0, 0.2),
     'L0_ffn_ln_b': (0.0, 0.532),
     'L0_ffn_bn_g': (1.0, 0.6),
     'L0_ffn_bn_b': (0.0, 2.0),
     'L0_ffn_bn_var': (1.0, 0.6),
     'L0_ffn_br': (0.0, 0.8),
     'L0_ffn_b_down': (0.0, 0.1),
     'L0_ffn_b_up': (0.0, 0.1)}
    factors = {'L0_attn_bg': 5.764, 'L0_ffn_bn_mean': 64.0, 'L0_ffn_Wr': 8.0}
    for name, (base, spread) in spreads.items():
        noise = np.random.default_rng([zlib.crc32(name.encode()), seed]).standard_normal(out[name].shape)
        drawn = base * np.exp(spread * noise) if base else spread * noise
        out[name] = jnp.asarray(drawn.astype(out[name].dtype))
    for name, factor in factors.items():
        out[name] = (out[name] * factor).astype(out[name].dtype)
    return out
```

```python
from collections import namedtuple
from contextlib import ExitStack

import concourse.bass as bass
from concourse import mybir

ALU = mybir.AluOpType
ACT = mybir.ActivationFunctionType
AX = mybir.AxisListType
F32 = mybir.dt.float32
F16 = mybir.dt.float16
I32 = mybir.dt.int32

P = 128
EPS = 1e-5
X_SCALE = 2.0 ** 11
W_SCALE = 2.0 ** 8
H_SCALE = 2.0 ** 6
Q_W = 1 / (X_SCALE * W_SCALE)
GATE, DECAY, VALUE = range(3)
KINDS = (GATE, DECAY, VALUE)
STEPS = 24
BANKS = 3
CHUNK = 512

Batch = namedtuple("Batch", "n par")


def mixer_kernel(nc, x, Wg, bg, Wv, bv, Wd, bd, gate_W, ln_g, ln_b, bn_g, bn_b, bn_mean, bn_var,
                 Wr, br, W_down, b_down, W_up, b_up, out):
    B, S, D = x.shape
    M = Wg.shape[0]
    E, _, H = W_down.shape
    KT = D // P
    T = S // P
    C = S // CHUNK
    PLANES = M * KT
    EVAC = PLANES * 3 * C
    ADDS = PLANES - KT
    assert KT == 2 and T == 8 and C == 2 and M == 4 and 2 * H == P and PLANES * 3 == STEPS
    assert EVAC % BANKS == 0 and B % 2 == 0

    BIAS = {GATE: 0, VALUE: PLANES, DECAY: 2 * PLANES}
    LN_G, LN_B, BN_G, BN_B, BN_MEAN, BN_VAR = (3 * PLANES + KT * j for j in range(6))
    B_DOWN = BN_VAR + KT
    VECS = B_DOWN + E
    UP1 = KT * 2 * P
    UP2 = UP1 + D
    HB = UP2 + D
    EXPERT = HB + 2

    x_t = x.rearrange("b (t p) d -> b p t d", p=P)
    out_t = out.rearrange("b (t p) d -> b p t d", p=P)
    comb_dram = nc.dram_tensor("comb_dram", [2, M * S], F32, kind="Internal").ap()

    with ExitStack() as ctx:
        def sb(name, shape, dt=F32):
            return ctx.enter_context(nc.sbuf_tensor(name, shape, dt))

        def sem(name):
            return ctx.enter_context(nc.semaphore(name))

        w_hi = sb("w_hi", [P, M * 3, KT, D], F16)
        w_lo = sb("w_lo", [P, M * 3, KT, D], F16)
        w_stage = sb("w_stage", [P, 2, 3, KT, D])
        gw_stage = sb("gw_stage", [P, KT, M])
        gw_hi = sb("gw_hi", [P, KT, M], F16)
        gw_lo = sb("gw_lo", [P, KT, M], F16)
        vec_rows = sb("vec_rows", [VECS, P])
        vecs = sb("vecs", [P, VECS])
        experts = sb("experts", [P, E, EXPERT], F16)
        expert = sb("expert", [P, EXPERT], F16)
        wr = sb("wr", [P, KT, E])
        br_all = sb("br_all", [P, E])
        ident = sb("ident", [P, P])
        ones = sb("ones", [P, P])
        neg_half = sb("neg_half", [P, T])
        rank_init = sb("rank_init", [P, T, M])
        order8 = sb("order8", [P, E])
        route_mul = sb("route_mul", [P, KT])
        route_add = sb("route_add", [P, KT])
        small = sb("small", [P, 8, KT])
        x_in = sb("x_in", [P, 2, T, D])
        resid = sb("resid", [P, T, D])
        normed = sb("normed", [P, T, D])
        xh = sb("xh", [P, 2, KT, S], F16)
        xl = sb("xl", [P, 2, KT, S], F16)
        u_split = sb("u_split", [P, 2, KT, S], F16)
        uh, ul = u_split[:, 0], u_split[:, 1]
        gate_s = sb("gate_s", [P, 2, S])
        value_s = sb("value_s", [P, 2, S])
        decay_s = sb("decay_s", [P, 2, S])
        hid = sb("hid", [P, 4, S])
        acc = sb("acc", [P, 2, KT, S])
        comb_all = sb("comb_all", [P, M, S])
        h32 = sb("h32", [P, S])
        up_in1 = sb("up_in1", [P, S], F16)
        up_in2 = sb("up_in2", [P, S], F16)
        down_stage = u_split[:].bitcast(F32).rearrange("p a k (e j) -> p (a k e) j", j=P).rearrange(
            "p (e k) j -> p e k j", k=KT)
        up_stage = resid[:]
        up_bias_stage = acc[:, 1].rearrange("p a (e j) -> p (a e) j", j=D)
        stats = {k: sb("stats_" + k, [P, T, 6]) for k in "xaty"}
        moments = {k: sb("moments_" + k, [P, 5, T]) for k in "xaty"}
        root_in = {k: sb("root_in_" + k, [P, T]) for k in "xaty"}
        root = {k: sb("root_" + k, [P, T]) for k in "xaty"}
        mul_by = {k: sb("mul_by_" + k, [P, T]) for k in "xty"}
        add_to = {k: sb("add_to_" + k, [P, T]) for k in "xty"}
        shift_a = sb("shift_a", [P, T])
        logit = sb("logit", [P, T, M])
        beats = sb("beats", [P, 6, T])
        rank = sb("rank", [P, T, M])
        chosen = sb("chosen", [P, T, M])
        chosen_logit = sb("chosen_logit", [P, T, M])
        pair_sum = sb("pair_sum", [P, T])
        margin = sb("margin", [P, T, M])
        share = sb("share", [P, T, M])
        comb = sb("comb", [P, M, T])
        comb_rows = sb("comb_rows", [M * T, P])
        u_sums = sb("u_sums", [P, KT, C])
        z_mean = sb("z_mean", [P, 3, KT])
        z_all = sb("z_all", [P, KT, P])
        r8 = sb("r8", [P, 8, E])
        r1 = sb("r1", [P, 8])
        index = sb("index", [P, 1], I32)

        ps_main = ctx.enter_context(nc.psum_tensor("ps_main", [P, BANKS, CHUNK], F32))
        ps_aux = ctx.enter_context(nc.psum_tensor("ps_aux", [P, 4, CHUNK], F32))
        ps_misc = ctx.enter_context(nc.psum_tensor("ps_misc", [P, CHUNK], F32))
        ps_gates = ps_misc[:, 0:T * M]
        ps_route = ps_misc[:, 64:64 + E]
        ps_comb = ps_misc[0:M * T, P:2 * P]
        ps_vecs = ps_misc[:, 0:VECS]
        ps_bias = ps_misc[:, 64:64 + E]
        ps_tok = ps_aux[:].rearrange("p b (a d) -> p (b a) d", a=2)

        vecs_loaded, gw_loaded, misc_loaded = sem("vecs_loaded"), sem("gw_loaded"), sem("misc_loaded")
        w_loaded = [sem(f"w_loaded{m}") for m in range(M)]
        experts_loaded = sem("experts_loaded")
        rows_zero, pool_consts = sem("rows_zero"), sem("pool_consts")
        consts, ident_zero, ident_ready = sem("consts"), sem("ident_zero"), sem("ident_ready")
        vecs_turned, vecs_ready = sem("vecs_turned"), sem("vecs_ready")
        w_hi_ready, w_lo_ready = sem("w_hi_ready"), sem("w_lo_ready")
        bn_root_in, bn_root, prep_link = sem("bn_root_in"), sem("bn_root"), sem("prep_link")
        bias_turned, experts_ready = sem("bias_turned"), sem("experts_ready")
        main_filled = sem("main_filled")
        main_read = sem("main_read")
        decay_ready = sem("decay_ready")
        input_ready = sem("input_ready")
        scanned = sem("scanned")
        weighed = sem("weighed")
        summed = sem("summed")
        x_loaded = sem("x_loaded")
        x_link = sem("x_link")
        x_root_in, x_root, x_scale = sem("x_root_in"), sem("x_root"), sem("x_scale")
        x_normed, x_turned = sem("x_normed"), sem("x_turned")
        xh_ready, xl_ready = sem("xh_ready"), sem("xl_ready")
        gates_done, mix_link, margin_ready = sem("gates_done"), sem("mix_link"), sem("margin_ready")
        share_ready, comb_ready, comb_turned = sem("share_ready"), sem("comb_ready"), sem("comb_turned")
        comb_copied, comb_saved = sem("comb_copied"), sem("comb_saved")
        comb_loaded = [sem(f"comb_loaded{m}") for m in range(M)]
        a_turned, a_link, a_root_in, a_root = sem("a_turned"), sem("a_link"), sem("a_root_in"), sem("a_root")
        t_free, t_ready, t_link = sem("t_free"), sem("t_ready"), sem("t_link")
        t_root_in, t_root, u_scale, u_ready, u_turned = (
            sem("t_root_in"), sem("t_root"), sem("u_scale"), sem("u_ready"), sem("u_turned"))
        uh_ready, ul_ready = sem("uh_ready"), sem("ul_ready")
        route_link, z_ready, route_done = sem("route_link"), sem("z_ready"), sem("route_done")
        delta_ready, sig_ready, index_ready = sem("delta_ready"), sem("sig_ready"), sem("index_ready")
        expert_loaded, down_done, h_ready = sem("expert_loaded"), sem("down_done"), sem("h_ready")
        hh_ready, up_in_ready, up_done = sem("hh_ready"), sem("up_in_ready"), sem("up_done")
        y_link, y_root_in, y_root = sem("y_link"), sem("y_root_in"), sem("y_root")
        index_seen = sem("index_seen")
        out_ready, out_stored = sem("out_ready"), sem("out_stored")

        MIX_LINKS, ROUTE_LINKS, STAT_LINKS, Y_LINKS = 11, 12, 4, 7

        def iterations(eng, run):
            def turn(j, r):
                return Batch(2 * j + r, r % 2)
            run(turn(0, 0), turn(0, 1), None)
            with eng.Fori(0, B // 2 - 1) as j:
                for r in (1, 2):
                    run(turn(j, r), turn(j, r + 1), turn(j, r - 1))
            run(turn(0, B - 1), None, turn(0, B - 2))
            run(None, None, turn(0, B - 1))

        def chunk(c):
            return slice(c * CHUNK, (c + 1) * CHUNK)

        def tile(t):
            return slice(t * P, (t + 1) * P)

        block = ctx.enter_context(nc.Block())

        @block.sync
        def _(sp):
            def load_mixer(m):
                for j, w in enumerate((Wg, Wd, Wv)):
                    sp.dma_start(w_stage[:, m % 2, j], w[m].rearrange("(k p) e -> p k e", p=P)
                                 ).then_inc(w_loaded[m], 16)

            def load_comb(nx, m):
                sp.dma_start(comb_all[:, m, :],
                             comb_dram[nx.par, m * S:(m + 1) * S].rearrange("(a s) -> a s", a=1)
                             .broadcast_to([P, S])).then_inc(comb_loaded[m], 16)

            def save_comb(nx):
                sp.wait_ge(comb_copied, nx.n + 1)
                sp.dma_start(comb_dram[nx.par].rearrange("(r p) -> r p", p=P), comb_rows[:]
                             ).then_inc(comb_saved, 16)
                sp.wait_ge(comb_saved, 16 * nx.n + 16)

            sp.sem_inc(t_free, 1)
            sp.dma_start(x_in[:, 0], x_t[0]).then_inc(x_loaded, 16)
            row = 0
            for v in (bg, bv, bd):
                sp.dma_start(vec_rows[row:row + PLANES, :], v.rearrange("m (k p) -> (m k) p", p=P)
                             ).then_inc(vecs_loaded, 16)
                row += PLANES
            for v in (ln_g, ln_b, bn_g, bn_b, bn_mean, bn_var):
                sp.dma_start(vec_rows[row:row + KT, :], v.rearrange("(k p) -> k p", p=P)
                             ).then_inc(vecs_loaded, 16)
                row += KT
            for a in range(2):
                sp.dma_start(vec_rows[row:row + E, a * H:(a + 1) * H], b_down).then_inc(vecs_loaded, 16)
            load_mixer(0)
            sp.dma_start(gw_stage[:], gate_W.rearrange("(k p) m -> p k m", p=P)).then_inc(gw_loaded, 16)
            load_mixer(1)
            sp.dma_start(wr[:], Wr.rearrange("(k p) e -> p k e", p=P)).then_inc(misc_loaded, 16)
            sp.dma_start(br_all[:], br.rearrange("(a e) -> a e", a=1).broadcast_to([P, E])).then_inc(misc_loaded, 16)
            for k in range(KT):
                for a in range(2):
                    sp.dma_start(down_stage[:, :, k, a * H:(a + 1) * H],
                                 W_down[:, k * P:(k + 1) * P, :].rearrange("e p h -> p e h")
                                 ).then_inc(experts_loaded, 16)
            for a in range(2):
                sp.dma_start(up_stage[a * H:(a + 1) * H], W_up.rearrange("e h d -> h e d")
                             ).then_inc(experts_loaded, 16)
            for row in (64, 96):
                sp.dma_start(up_bias_stage[row:row + 1], b_up.rearrange("(a e) d -> a e d", a=1)
                             ).then_inc(experts_loaded, 16)
            for m in (2, 3):
                sp.wait_ge(w_hi_ready, m - 1)
                sp.wait_ge(w_lo_ready, m - 1)
                load_mixer(m)
                if m == 2:
                    save_comb(Batch(0, 0))
                    for mm in range(M):
                        load_comb(Batch(0, 0), mm)

            def run(bt, nx, pv):
                if nx:
                    if pv:
                        sp.wait_ge(t_ready, pv.n + 1)
                    else:
                        sp.wait_ge(x_root_in, 1)
                    sp.dma_start(x_in[:, nx.par], x_t[bass.ds(nx.n, 1)].rearrange("a p t d -> p (a t) d")
                                 ).then_inc(x_loaded, 16)
                if pv:
                    sp.wait_ge(experts_ready, 6)
                    sp.wait_ge(index_ready, 2 * pv.n + 2)
                    sp.sem_inc(index_seen, 1)
                    e = sp.value_load(index[0:1, 0:1], min_val=0, max_val=E - 1)
                    sp.dma_start(expert[:].bitcast(I32),
                                 experts[:].bitcast(I32)[:, bass.ds(e, 1), :].rearrange("p a c -> p (a c)")
                                 ).then_inc(expert_loaded, 16)
                if nx:
                    save_comb(nx)
                    for m in range(M - 1):
                        sp.wait_ge(weighed, PLANES * bt.n + KT * (m + 1))
                        load_comb(nx, m)
                if pv:
                    sp.wait_ge(out_ready, pv.n + 1)
                    sp.dma_start(out_t[bass.ds(pv.n, 1)].rearrange("a p t d -> p (a t) d"), resid[:]
                                 ).then_inc(out_stored, 16)
                    sp.wait_ge(out_stored, 16 * pv.n + 16)
                    sp.sem_inc(t_free, 1)
                if nx:
                    sp.wait_ge(weighed, PLANES * bt.n + PLANES)
                    load_comb(nx, M - 1)

            iterations(sp, run)

        @block.gpsimd
        def _(pool):
            pool.memset(ident[:], 0.0).then_inc(ident_zero, 1)
            pool.wait_ge(ident_zero, 1)
            pool.affine_select(out=ident[:], in_=ident[:], compare_op=ALU.not_equal, fill=1.0, base=0,
                               pattern=[[-1, P]], channel_multiplier=1).then_inc(ident_ready, 1)
            pool.memset(neg_half[:], -0.5).then_inc(pool_consts, 1)
            pool.memset(ones[:], 1.0).then_inc(pool_consts, 1)
            for m in range(M):
                pool.memset(rank_init[:, :, m], float(M - 1 - m)).then_inc(pool_consts, 1)
            for e in range(E):
                pool.memset(order8[:, e:e + 1], float(E - e)).then_inc(pool_consts, 1)

            def power(key, ready, done, n):
                pool.wait_ge(ready, n + 1)
                pool.tensor_tensor(root[key][:], root_in[key][:], neg_half[:], ALU.pow).then_inc(done, 1)

            pool.wait_ge(pool_consts, 2 + M + E)
            power("x", x_root_in, x_root, 0)
            pool.wait_ge(bn_root_in, 1)
            pool.tensor_tensor(small[:, 1], small[:, 0], neg_half[:, 0:KT], ALU.pow).then_inc(bn_root, 1)

            def multiply(bt, p):
                pool.wait_ge(main_read, EVAC * bt.n + 6 * p + 6)
                pool.tensor_tensor(value_s[:, p % 2], gate_s[:, p % 2], value_s[:, p % 2], ALU.mult
                                   ).then_inc(input_ready, 1)

            def add(bt, p):
                pool.wait_ge(weighed, PLANES * bt.n + p + 1)
                if p >= 2 * KT:
                    pool.wait_ge(summed, ADDS * bt.n + p - 2 * KT + 1)
                a = acc[:, bt.par, p % KT]
                pool.tensor_tensor(a, a, hid[:, p % 4], ALU.add).then_inc(summed, 1)

            def run(bt, nx, pv):
                for s in range(STEPS):
                    p, k = divmod(s, 3)
                    if k == 0:
                        if p >= 2 + KT and bt:
                            add(bt, p - 2)
                        if p < 2 and pv:
                            add(pv, PLANES - 2 + p)
                    if k == 2 and bt:
                        multiply(bt, p)
                    if s == 7 and pv:
                        power("a", a_root_in, a_root, pv.n)
                    if s == 10 and pv:
                        power("t", t_root_in, t_root, pv.n)
                    if s == 13 and nx:
                        power("x", x_root_in, x_root, nx.n)
                    if s == 22 and pv:
                        power("y", y_root_in, y_root, pv.n)

            iterations(pool, run)

        @block.scalar
        def _(act):
            def mixer_high(m):
                act.wait_ge(w_loaded[m], 48)
                act.activation(w_hi[:, 3 * m:3 * m + 3], w_stage[:, m % 2], ACT.Copy, scale=W_SCALE
                               ).then_inc(w_hi_ready, 1)

            def normalise_x(nx, first):
                act.wait_ge(x_scale, 2 * nx.n + 2)
                for t in range(T):
                    ins = act.activation(normed[:, t], x_in[:, nx.par, t], ACT.Identity,
                                         bias=add_to["x"][:, t:t + 1], scale=mul_by["x"][:, t:t + 1])
                ins.then_inc(x_normed, 1)

            def high_x(nx):
                act.wait_ge(x_turned, nx.n + 1)
                for k in range(KT):
                    for c in range(C):
                        act.activation(xh[:, nx.par, k, chunk(c)], ps_aux[:, C * k + c], ACT.Copy
                                       ).then_inc(xh_ready, 1)

            def shares(nx):
                act.wait_ge(margin_ready, nx.n + 1)
                act.activation(share[:], margin[:], ACT.Sigmoid).then_inc(share_ready, 1)

            def evacuate(bt, p, kind, first):
                m, half = divmod(p, KT)
                col = BIAS[kind] + KT * m + half
                if kind == GATE and not (first and p < 2):
                    act.wait_ge(input_ready, PLANES * bt.n + p - 1)
                if kind == DECAY and not (first and p < 2):
                    act.wait_ge(scanned, PLANES * bt.n + p - 1)
                buf = {GATE: gate_s, DECAY: decay_s, VALUE: value_s}[kind]
                for c in range(C):
                    n = 6 * p + 2 * kind + c
                    act.wait_ge(main_filled, EVAC * bt.n + n + 1)
                    act.activation(buf[:, p % 2, chunk(c)], ps_main[:, n % BANKS],
                                   ACT.Tanh if kind == VALUE else ACT.Sigmoid,
                                   bias=vecs[:, col:col + 1], scale=Q_W).then_inc(main_read, 1)
                if kind == VALUE:
                    act.wait_ge(main_read, EVAC * bt.n + 6 * p + 4)
                    act.activation(decay_s[:, p % 2], decay_s[:, p % 2], ACT.Copy, bias=0.001, scale=0.998
                                   ).then_inc(decay_ready, 1)

            def normalise_t(pv):
                act.wait_ge(u_scale, 2 * pv.n + 2)
                for t in range(T):
                    ins = act.activation(normed[:, t], resid[:, t], ACT.Identity,
                                         bias=add_to["t"][:, t:t + 1], scale=mul_by["t"][:, t:t + 1])
                ins.then_inc(u_ready, 1)

            def high_u(pv):
                act.wait_ge(u_turned, pv.n + 1)
                for k in range(KT):
                    for c in range(C):
                        act.activation(uh[:, k, chunk(c)], ps_aux[:, C * k + c], ACT.Copy,
                                       accum_out=u_sums[:, k, c:c + 1]).then_inc(uh_ready, 1)

            def router_sigmoids(pv):
                act.wait_ge(delta_ready, pv.n + 1)
                act.activation(r8[:, 1], r8[:, 0], ACT.Sigmoid)
                act.activation(r8[:, 2], r8[:, 0], ACT.Sigmoid, scale=-1.0).then_inc(sig_ready, 1)

            def hidden(pv):
                act.wait_ge(down_done, pv.n + 1)
                for c in range(C):
                    act.activation(h32[:, chunk(c)], ps_aux[:, c], ACT.Relu,
                                   bias=expert[:, HB:HB + 2].bitcast(F32), scale=Q_W * H_SCALE
                                   ).then_inc(h_ready, 1)
                for c in range(C):
                    act.wait_ge(h_ready, C * pv.n + c + 1)
                    act.activation(up_in1[:, chunk(c)], h32[:, chunk(c)], ACT.Copy).then_inc(hh_ready, 1)

            mixer_high(0)
            act.wait_ge(gw_loaded, 16)
            act.activation(gw_hi[:], gw_stage[:], ACT.Copy, scale=W_SCALE).then_inc(w_hi_ready, 1)
            first = Batch(0, 0)
            normalise_x(first, True)
            high_x(first)
            mixer_high(1)
            shares(first)
            act.wait_ge(vecs_ready, 1)

            def run(bt, nx, pv):
                for s in range(STEPS):
                    p, kind = divmod(s, 3)
                    if bt:
                        evacuate(bt, p, kind, pv is None)
                    if not pv and s in (2, 8):
                        mixer_high(2 + (s == 8))
                    if pv:
                        if s == 11:
                            normalise_t(pv)
                        if s == 13:
                            high_u(pv)
                        if s == 16:
                            router_sigmoids(pv)
                        if s == 19:
                            hidden(pv)
                    if nx:
                        if s == 14:
                            if pv:
                                act.wait_ge(u_turned, pv.n + 1)
                            else:
                                act.wait_ge(x_turned, 1)
                            normalise_x(nx, False)
                        if s == 16:
                            high_x(nx)
                        if s == 18:
                            shares(nx)

            iterations(act, run)

        @block.vector
        def _(dve):
            def linker(sem_, base):
                count = [0]

                def link(ins):
                    count[0] += 1
                    ins.then_inc(sem_, 1)
                    dve.wait_ge(sem_, base + count[0])
                link.count = count
                return link

            def moments_of(key, rows, link):
                for t in range(T):
                    ins = dve.bn_stats(out=stats[key][:, t], in_=rows(t))
                link(ins)
                even, odd = stats[key][:, :, 0:3], stats[key][:, :, 3:6]
                mom = moments[key]
                dve.tensor_tensor(mom[:, 0], even[:, :, 1], odd[:, :, 1], ALU.add)
                dve.tensor_tensor(mom[:, 1], even[:, :, 2], odd[:, :, 2], ALU.add)
                link(dve.tensor_tensor(mom[:, 2], even[:, :, 1], odd[:, :, 1], ALU.subtract))
                link(dve.tensor_tensor(mom[:, 3], mom[:, 2], mom[:, 2], ALU.mult))
                link(dve.scalar_tensor_tensor(mom[:, 4], mom[:, 3], D / 4, mom[:, 1], ALU.mult, ALU.add))

            def mixer_low(m):
                dve.wait_ge(w_hi_ready, m + 1 + (m > 0))
                dve.scalar_tensor_tensor(w_lo[:, 3 * m:3 * m + 3].rearrange("p a k e -> p (a k e)"),
                                         w_stage[:, m % 2].rearrange("p a k e -> p (a k e)"), W_SCALE,
                                         w_hi[:, 3 * m:3 * m + 3].rearrange("p a k e -> p (a k e)"),
                                         ALU.mult, ALU.subtract).then_inc(w_lo_ready, 1)

            def x_moments(nx):
                dve.wait_ge(x_loaded, 16 * nx.n + 16)
                link = linker(x_link, STAT_LINKS * nx.n)
                moments_of("x", lambda t: x_in[:, nx.par, t], link)
                assert link.count[0] == STAT_LINKS
                dve.tensor_scalar(root_in["x"][:], moments["x"][:, 4], 1 / D, EPS, ALU.mult, ALU.add
                                  ).then_inc(x_root_in, 1)

            def scales(key, root_ready, n, done):
                dve.wait_ge(root_ready, n + 1)
                dve.tensor_scalar(mul_by[key][:], root[key][:], X_SCALE, None, ALU.mult).then_inc(done, 1)
                dve.wait_ge(done, 2 * n + 1)
                dve.scalar_tensor_tensor(add_to[key][:], moments[key][:, 0], -0.5, mul_by[key][:],
                                         ALU.mult, ALU.mult).then_inc(done, 1)

            def low_x(nx):
                for k in range(KT):
                    for c in range(C):
                        dve.wait_ge(xh_ready, KT * C * nx.n + C * k + c + 1)
                        dve.tensor_tensor(xl[:, nx.par, k, chunk(c)], ps_aux[:, C * k + c],
                                          xh[:, nx.par, k, chunk(c)], ALU.subtract).then_inc(xl_ready, 1)

            def rank_mixers(nx):
                link = linker(mix_link, MIX_LINKS * nx.n)
                dve.wait_ge(gates_done, nx.n + 1)
                link(dve.tensor_scalar(logit[:], ps_gates.rearrange("p (t m) -> p t m", m=M), Q_W, None, ALU.mult))
                b = beats[:].rearrange("p c t -> p t c")
                at = 0
                parts = []
                for d in range(1, M):
                    n = M - d
                    ins = dve.tensor_tensor(b[:, :, at:at + n], logit[:, :, 0:n], logit[:, :, d:M], ALU.is_ge)
                    parts.append((d, n, at))
                    at += n
                link(ins)
                src = rank_init
                for d, n, at in parts:
                    if d == 1:
                        dve.tensor_copy(rank[:, :, M - 1:M], rank_init[:, :, M - 1:M])
                    link(dve.tensor_tensor(rank[:, :, 0:n], src[:, :, 0:n], b[:, :, at:at + n], ALU.subtract))
                    link(dve.tensor_tensor(rank[:, :, d:M], rank[:, :, d:M], b[:, :, at:at + n], ALU.add))
                    src = rank
                link(dve.tensor_scalar(chosen[:], rank[:], 1.5, None, ALU.is_lt))
                link(dve.tensor_tensor(chosen_logit[:], chosen[:], logit[:], ALU.mult))
                link(dve.tensor_reduce(pair_sum[:], chosen_logit[:], AX.X, ALU.add))
                dve.scalar_tensor_tensor(margin[:], logit[:], 2.0, pair_sum[:].broadcast_to([P, T, M]),
                                         ALU.mult, ALU.subtract).then_inc(margin_ready, 1)
                return link

            def weights_of(nx):
                dve.wait_ge(share_ready, nx.n + 1)
                dve.tensor_tensor(comb[:].rearrange("p m t -> p t m"), share[:], chosen[:], ALU.mult
                                  ).then_inc(comb_ready, 1)

            def copy_weights(nx, first):
                dve.wait_ge(comb_turned, nx.n + 1)
                if not first:
                    dve.wait_ge(comb_saved, 16 * nx.n)
                dve.tensor_copy(comb_rows[:], ps_comb).then_inc(comb_copied, 1)

            def scan(bt, p, first):
                dve.wait_ge(decay_ready, PLANES * bt.n + p + 1)
                dve.wait_ge(input_ready, PLANES * bt.n + p + 1)
                if p >= 2 * KT + 2:
                    dve.wait_ge(summed, ADDS * bt.n + p - 5)
                elif p < 4 and not first:
                    dve.wait_ge(summed, ADDS * bt.n + p - 3)
                dve.tensor_tensor_scan(hid[:, p % 4], decay_s[:, p % 2], value_s[:, p % 2], 0.0,
                                       ALU.mult, ALU.add).then_inc(scanned, 1)

            def weigh(bt, p):
                m, half = divmod(p, KT)
                dve.wait_ge(scanned, PLANES * bt.n + p + 1)
                if half == 0:
                    dve.wait_ge(comb_loaded[m], 16 * bt.n + 16)
                dst = acc[:, bt.par, half] if m == 0 else hid[:, p % 4]
                dve.tensor_tensor(dst, hid[:, p % 4], comb_all[:, m], ALU.mult).then_inc(weighed, 1)

            def a_moments(pv):
                dve.wait_ge(a_turned, pv.n + 1)
                link = linker(a_link, STAT_LINKS * pv.n)
                moments_of("a", lambda t: ps_tok[:, t], link)
                dve.tensor_scalar(root_in["a"][:], moments["a"][:, 4], 1 / D, EPS, ALU.mult, ALU.add
                                  ).then_inc(a_root_in, 1)

            def residual(pv):
                dve.wait_ge(a_root, pv.n + 1)
                dve.wait_ge(t_free, pv.n + 1)
                link = linker(t_link, STAT_LINKS * pv.n)
                dve.scalar_tensor_tensor(shift_a[:], moments["a"][:, 0], 0.5, root["a"][:], ALU.mult, ALU.mult)
                for t in range(T):
                    ins = dve.scalar_tensor_tensor(resid[:, t], ps_tok[:, t], root["a"][:, t:t + 1],
                                                   x_in[:, pv.par, t], ALU.mult, ALU.add)
                ins.then_inc(t_ready, 1)
                dve.wait_ge(t_ready, pv.n + 1)
                moments_of("t", lambda t: resid[:, t], link)
                dve.tensor_scalar(root_in["t"][:], moments["t"][:, 4], (1.0 + EPS) / D, EPS * EPS, ALU.mult, ALU.add
                                  ).then_inc(t_root_in, 1)

            def low_u(pv):
                for k in range(KT):
                    for c in range(C):
                        dve.wait_ge(uh_ready, KT * C * pv.n + C * k + c + 1)
                        dve.tensor_tensor(ul[:, k, chunk(c)], ps_aux[:, C * k + c], uh[:, k, chunk(c)],
                                          ALU.subtract).then_inc(ul_ready, 1)

            def route_in(pv):
                link = linker(route_link, ROUTE_LINKS * pv.n)
                link(dve.tensor_tensor(z_mean[:, 0], u_sums[:, :, 0], u_sums[:, :, 1], ALU.add))
                link(dve.tensor_tensor(z_mean[:, 1], z_mean[:, 0], route_mul[:], ALU.mult))
                link(dve.tensor_tensor(z_mean[:, 2], z_mean[:, 1], route_add[:], ALU.add))
                for k in range(KT):
                    ins = dve.tensor_scalar(z_all[:, k], ones[:], z_mean[:, 2, k:k + 1], None, ALU.mult)
                ins.then_inc(z_ready, 1)

            def route_logits(pv):
                link = linker(route_link, ROUTE_LINKS * pv.n + 3)
                dve.wait_ge(route_done, pv.n + 1)
                link(dve.tensor_tensor(r8[:, 3], ps_route, br_all[:], ALU.add))
                link(dve.tensor_reduce(r1[:, 0:1], r8[:, 3], AX.X, ALU.max))
                dve.tensor_scalar(r8[:, 0], r8[:, 3], r1[:, 0:1], None, ALU.subtract).then_inc(delta_ready, 1)

            def route_pick(pv):
                link = linker(route_link, ROUTE_LINKS * pv.n + 5)
                dve.wait_ge(sig_ready, pv.n + 1)
                link(dve.reciprocal(r8[:, 4], r8[:, 2]))
                link(dve.tensor_tensor(r8[:, 5], r8[:, 4], r8[:, 1], ALU.mult))
                link(dve.tensor_reduce(r1[:, 1:2], r8[:, 5], AX.X, ALU.add))
                link(dve.reciprocal(r1[:, 2:3], r1[:, 1:2]))
                link(dve.tensor_scalar(r8[:, 6], r8[:, 5], r1[:, 2:3], None, ALU.mult))
                link(dve.tensor_reduce(r1[:, 3:4], r8[:, 6], AX.X, ALU.max))
                link(dve.scalar_tensor_tensor(r8[:, 7], r8[:, 6], r1[:, 3:4], order8[:], ALU.is_equal, ALU.mult))
                dve.tensor_reduce(r1[:, 4:5], r8[:, 7], AX.X, ALU.max).then_inc(index_ready, 1)
                dve.wait_ge(index_ready, 2 * pv.n + 1)
                dve.tensor_scalar(index[:], r1[:, 4:5], -1.0, float(E), ALU.mult, ALU.add).then_inc(index_ready, 1)
                dve.tensor_scalar(r1[:, 5:6], r1[:, 3:4], 1 / (H_SCALE * W_SCALE), None, ALU.mult)
                return link

            def low_h(pv):
                dve.wait_ge(hh_ready, C * pv.n + C)
                dve.tensor_copy(up_in2[0:H, :], up_in1[0:H, :])
                dve.tensor_tensor(up_in1[H:P, :], h32[H:P, :], up_in1[H:P, :], ALU.subtract
                                  ).then_inc(up_in_ready, 1)

            def y_moments(pv):
                link = linker(y_link, Y_LINKS * pv.n)
                dve.wait_ge(up_done, pv.n + 1)
                dve.scalar_tensor_tensor(r1[:, 6:7], r1[:, 5:6], 1 / D, r1[:, 5:6], ALU.mult, ALU.mult)
                moments_of("y", lambda t: ps_tok[:, t], link)
                dve.tensor_scalar(root_in["y"][:], moments["y"][:, 4], r1[:, 6:7], EPS, ALU.mult, ALU.add
                                  ).then_inc(y_root_in, 1)

            def finish(pv):
                link = linker(y_link, Y_LINKS * pv.n + STAT_LINKS)
                dve.wait_ge(y_root, pv.n + 1)
                link(dve.tensor_scalar(mul_by["y"][:], root["y"][:], r1[:, 5:6], None, ALU.mult))
                dve.scalar_tensor_tensor(add_to["y"][:], moments["y"][:, 0], 0.5, mul_by["y"][:], ALU.mult, ALU.mult)
                for t in range(T):
                    ins = dve.scalar_tensor_tensor(resid[:, t], ps_tok[:, t], mul_by["y"][:, t:t + 1],
                                                   resid[:, t], ALU.mult, ALU.add)
                link(ins)
                link(dve.tensor_tensor(add_to["y"][:], add_to["y"][:], shift_a[:], ALU.add))
                for t in range(T):
                    ins = dve.tensor_scalar(resid[:, t], resid[:, t], add_to["y"][:, t:t + 1], None, ALU.subtract)
                ins.then_inc(out_ready, 1)

            first = Batch(0, 0)
            dve.memset(up_in2[H:P, :], 0.0)
            dve.memset(experts[H:P, :, UP2:HB], 0.0).then_inc(rows_zero, 1)
            dve.wait_ge(rows_zero, 1)
            for row in (64, 96):
                dve.memset(up_in2[row:row + 1, :], H_SCALE).then_inc(consts, 1)
            x_moments(first)
            scales("x", x_root, 0, x_scale)
            mixer_low(0)
            dve.wait_ge(w_hi_ready, 2)
            dve.scalar_tensor_tensor(gw_lo[:], gw_stage[:], W_SCALE, gw_hi[:], ALU.mult, ALU.subtract
                                     ).then_inc(consts, 1)
            dve.wait_ge(vecs_turned, 1)
            dve.tensor_copy(vecs[:], ps_vecs).then_inc(vecs_ready, 1)
            low_x(first)
            dve.wait_ge(pool_consts, 2 + M + E)
            rank_mixers(first)
            mixer_low(1)
            weights_of(first)
            copy_weights(first, True)

            def prepare_router():
                link = linker(prep_link, 0)
                dve.wait_ge(vecs_ready, 1)
                v = {k: vecs[:, c:c + KT] for k, c in (("g", LN_G), ("b", LN_B), ("bg", BN_G), ("bb", BN_B),
                                                       ("mean", BN_MEAN), ("var", BN_VAR))}
                dve.tensor_scalar(small[:, 0], v["var"], EPS, None, ALU.add).then_inc(bn_root_in, 1)
                dve.wait_ge(bn_root, 1)
                link(dve.tensor_tensor(small[:, 2], small[:, 1], v["bg"], ALU.mult))
                link(dve.tensor_tensor(small[:, 3], v["b"], v["mean"], ALU.subtract))
                link(dve.tensor_tensor(small[:, 4], small[:, 3], small[:, 2], ALU.mult))
                link(dve.tensor_tensor(route_add[:], small[:, 4], v["bb"], ALU.add))
                link(dve.scalar_tensor_tensor(route_mul[:], small[:, 2], 1 / (X_SCALE * S), v["g"], ALU.mult, ALU.mult))
                return link

            def prepare_experts(link):
                dve.wait_ge(experts_loaded, 16 * 8)
                link(dve.tensor_scalar(small[:, 5], vecs[:, LN_G:LN_G + KT], W_SCALE, None, ALU.mult))
                for k in range(KT):
                    hi = experts[:, :, (2 * k) * P:(2 * k + 1) * P]
                    lo = experts[:, :, (2 * k + 1) * P:(2 * k + 2) * P]
                    link(dve.tensor_scalar(hi, down_stage[:, :, k], small[:, 5, k:k + 1], None, ALU.mult))
                    dve.scalar_tensor_tensor(lo, down_stage[:, :, k], small[:, 5, k:k + 1], hi,
                                             ALU.mult, ALU.subtract).then_inc(experts_ready, 1)
                up1 = experts[:, :, UP1:UP2]
                up2 = experts[:, :, UP2:HB]
                link(dve.tensor_scalar(up1, up_stage, W_SCALE, None, ALU.mult))
                dve.scalar_tensor_tensor(up2[0:H], up_stage[0:H], W_SCALE, up1[0:H], ALU.mult, ALU.subtract
                                         ).then_inc(experts_ready, 1)
                for row in (64, 96):
                    r = slice(row, row + 1)
                    ins = dve.tensor_scalar(up2[r], up_bias_stage[r], W_SCALE, None, ALU.mult)
                    if row == 64:
                        ins.then_inc(experts_ready, 1)
                link(ins)
                dve.scalar_tensor_tensor(up2[r], up_bias_stage[r], W_SCALE, up2[r], ALU.mult, ALU.subtract
                                         ).then_inc(experts_ready, 1)
                dve.wait_ge(bias_turned, 1)
                link(dve.tensor_tensor(r8[:, 0], ps_bias, vecs[:, B_DOWN:B_DOWN + E], ALU.add))
                dve.tensor_scalar(experts[:, :, HB:HB + 2].bitcast(F32).rearrange("p e a -> p (e a)"), r8[:, 0],
                                  H_SCALE, None, ALU.mult).then_inc(experts_ready, 1)

            def run(bt, nx, pv):
                for s in range(STEPS):
                    p, k = divmod(s, 3)
                    at = (bt, p - 1) if p >= 1 else (pv, PLANES - 1)
                    if at[0] and k == 1:
                        scan(*at, pv is None)
                    if at[0] and k == 2:
                        weigh(*at)
                    if not pv:
                        if s == 2:
                            mixer_low(2)
                        if s == 3:
                            prep = prepare_router()
                        if s == 8:
                            mixer_low(3)
                        if s == 9:
                            prepare_experts(prep)
                    if pv:
                        if s == 5:
                            a_moments(pv)
                        if s == 8:
                            residual(pv)
                        if s == 11:
                            scales("t", t_root, pv.n, u_scale)
                        if s == 13:
                            low_u(pv)
                        if s == 14:
                            route_in(pv)
                        if s == 16:
                            route_logits(pv)
                            route_pick(pv)
                        if s == 19:
                            low_h(pv)
                        if s == 21:
                            y_moments(pv)
                        if s == 23:
                            finish(pv)
                    if nx:
                        if s == 12:
                            x_moments(nx)
                        if s == 14:
                            scales("x", x_root, nx.n, x_scale)
                        if s == 16:
                            low_x(nx)
                        if s == 18:
                            rank_mixers(nx)
                        if s == 19:
                            weights_of(nx)
                        if s == 20:
                            copy_weights(nx, False)

            iterations(dve, run)

        @block.tensor
        def _(pe):
            def turn_rows(rows_of, done):
                for k in range(KT):
                    for t in range(T):
                        ins = pe.transpose(ps_aux[:, C * k + t // 4, tile(t % 4)],
                                           normed[:, t, k * P:(k + 1) * P], ident[:])
                ins.then_inc(done, 1)

            def turn_x(nx):
                pe.wait_ge(x_normed, nx.n + 1)
                turn_rows(normed, x_turned)

            def gates(nx):
                pe.wait_ge(xh_ready, KT * C * (nx.n + 1))
                pe.wait_ge(xl_ready, KT * C * (nx.n + 1))
                for t in range(T):
                    n = 0
                    for k in range(KT):
                        for a, b in ((xh, gw_hi), (xh, gw_lo), (xl, gw_hi)):
                            ins = pe.matmul(ps_gates[:, M * t:M * (t + 1)], a[:, nx.par, k, tile(t)], b[:, k],
                                            start=(n == 0), stop=(n == 3 * KT - 1))
                            n += 1
                ins.then_inc(gates_done, 1)

            def turn_weights(nx):
                pe.wait_ge(comb_ready, nx.n + 1)
                pe.transpose(ps_comb, comb[:].rearrange("p m t -> p (m t)"), ident[:]).then_inc(comb_turned, 1)

            def product(bt, p, kind, first):
                m, half = divmod(p, KT)
                if kind == GATE and p == 0:
                    pe.wait_ge(xh_ready, KT * C * (bt.n + 1))
                    pe.wait_ge(xl_ready, KT * C * (bt.n + 1))
                if first and kind == GATE and half == 0:
                    pe.wait_ge(w_hi_ready, m + 1 + (m > 0))
                    pe.wait_ge(w_lo_ready, m + 1)
                for c in range(C):
                    n = 6 * p + 2 * kind + c
                    if not (first and n < BANKS):
                        pe.wait_ge(main_read, EVAC * bt.n + n - BANKS + 1)
                    i = 0
                    for k in range(KT):
                        for w, v in ((w_hi, xh), (w_lo, xh), (w_hi, xl)):
                            ins = pe.matmul(ps_main[:, n % BANKS], w[:, 3 * m + kind, k, half * P:(half + 1) * P],
                                            v[:, bt.par, k, chunk(c)], start=(i == 0), stop=(i == 3 * KT - 1))
                            i += 1
                    ins.then_inc(main_filled, 1)

            def turn_a(pv):
                pe.wait_ge(summed, ADDS * pv.n + ADDS)
                for t in range(T):
                    for k in range(KT):
                        ins = pe.transpose(ps_tok[:, t, k * P:(k + 1) * P], acc[:, pv.par, k, tile(t)], ident[:])
                ins.then_inc(a_turned, 1)

            def turn_u(pv):
                pe.wait_ge(u_ready, pv.n + 1)
                turn_rows(normed, u_turned)

            def route(pv):
                pe.wait_ge(z_ready, pv.n + 1)
                for k in range(KT):
                    ins = pe.matmul(ps_route, z_all[:, k], wr[:, k], start=(k == 0), stop=(k == KT - 1))
                ins.then_inc(route_done, 1)

            def down(pv):
                pe.wait_ge(expert_loaded, 16 * pv.n + 16)
                pe.wait_ge(ul_ready, KT * C * (pv.n + 1))
                for c in range(C):
                    i = 0
                    for k in range(KT):
                        for part, v in ((0, uh), (1, uh), (0, ul)):
                            ins = pe.matmul(ps_aux[:, c], expert[:, (2 * k + part) * P:(2 * k + part + 1) * P],
                                            v[:, k, chunk(c)], start=(i == 0), stop=(i == 3 * KT - 1))
                            i += 1
                ins.then_inc(down_done, 1)

            def up(pv):
                pe.wait_ge(up_in_ready, pv.n + 1)
                for t in range(T):
                    pe.matmul(ps_tok[:, t], up_in1[:, tile(t)], expert[:, UP1:UP2], start=True, stop=False)
                    ins = pe.matmul(ps_tok[:, t], up_in2[:, tile(t)], expert[:, UP2:HB], start=False, stop=True)
                ins.then_inc(up_done, 1)

            first = Batch(0, 0)
            pe.wait_ge(ident_ready, 1)
            pe.wait_ge(vecs_loaded, 16 * 11)
            pe.transpose(ps_vecs, vec_rows[:], ident[0:VECS, 0:VECS]).then_inc(vecs_turned, 1)
            turn_x(first)
            pe.wait_ge(vecs_ready, 1)
            pe.wait_ge(consts, 3)
            gates(first)
            turn_weights(first)

            def hidden_bias():
                pe.wait_ge(experts_loaded, 16 * 8)
                pe.wait_ge(misc_loaded, 32)
                pe.wait_ge(comb_copied, 1)
                for e in range(E):
                    for k in range(KT):
                        ins = pe.matmul(ps_bias[:, e:e + 1], down_stage[:, e, k], vecs[:, LN_B + k:LN_B + k + 1],
                                        start=(k == 0), stop=(k == KT - 1))
                ins.then_inc(bias_turned, 1)

            def run(bt, nx, pv):
                for s in range(STEPS):
                    p, kind = divmod(s, 3)
                    if not pv and s == 6:
                        hidden_bias()
                    if pv:
                        if s == 5:
                            turn_a(pv)
                        if s == 12:
                            turn_u(pv)
                        if s == 15:
                            route(pv)
                        if s == 18:
                            down(pv)
                        if s == 21:
                            up(pv)
                    if nx:
                        if s == 15:
                            if pv:
                                pe.wait_ge(ul_ready, KT * C * (pv.n + 1))
                            turn_x(nx)
                        if s == 17:
                            gates(nx)
                        if s == 20:
                            turn_weights(nx)
                    if bt:
                        product(bt, p, kind, pv is None)

            iterations(pe, run)


_INS = ["L0_attn_x", "L0_attn_Wg", "L0_attn_bg", "L0_attn_Wv", "L0_attn_bv", "L0_attn_Wd", "L0_attn_bd",
        "L0_attn_gate_W", "L0_ffn_ln_g", "L0_ffn_ln_b", "L0_ffn_bn_g", "L0_ffn_bn_b", "L0_ffn_bn_mean",
        "L0_ffn_bn_var", "L0_ffn_Wr", "L0_ffn_br", "L0_ffn_W_down", "L0_ffn_b_down", "L0_ffn_W_up",
        "L0_ffn_b_up"]


def kernel(**inputs):
    import numpy as np
    import concourse.bacc as bacc
    from concourse.bass_utils import run_bass_kernel_spmd

    nc = bacc.Bacc("TRN2", target_bir_lowering=False, num_devices=1)
    arrays, args = {}, []
    for name in _INS:
        a = np.ascontiguousarray(inputs[name])
        arrays[f"in_{name}"] = a
        args.append(nc.dram_tensor(f"in_{name}", a.shape, mybir.dt.from_np(a.dtype), kind="ExternalInput").ap())
    shape = inputs["L0_attn_x"].shape
    args.append(nc.dram_tensor("out", shape, F32, kind="ExternalOutput").ap())
    mixer_kernel(nc, *args)
    r = run_bass_kernel_spmd(nc, [arrays], core_ids=[0])
    return r.results[0]["out"]
```

```python
from collections import namedtuple
from contextlib import ExitStack

import concourse.bass as bass
from concourse import mybir

ALU = mybir.AluOpType
ACT = mybir.ActivationFunctionType
AX = mybir.AxisListType
F32 = mybir.dt.float32
F16 = mybir.dt.float16
I32 = mybir.dt.int32

P = 128
EPS = 1e-5
X_SCALE = 2.0 ** 11
W_SCALE = 2.0 ** 8
H_SCALE = 2.0 ** 6
Q_W = 1 / (X_SCALE * W_SCALE)
GATE, DECAY, VALUE = range(3)
KINDS = (GATE, DECAY, VALUE)
STEPS = 24
BANKS = 3
CHUNK = 512

Batch = namedtuple("Batch", "n par")


def mixer_kernel(nc, x, Wg, bg, Wv, bv, Wd, bd, gate_W, ln_g, ln_b, bn_g, bn_b, bn_mean, bn_var,
                 Wr, br, W_down, b_down, W_up, b_up, out):
    B, S, D = x.shape
    M = Wg.shape[0]
    E, _, H = W_down.shape
    KT = D // P
    T = S // P
    C = S // CHUNK
    PLANES = M * KT
    EVAC = PLANES * 3 * C
    ADDS = PLANES - KT
    assert KT == 2 and T == 8 and C == 2 and M == 4 and 2 * H == P and PLANES * 3 == STEPS
    assert EVAC % BANKS == 0 and B % 2 == 0

    BIAS = {GATE: 0, VALUE: PLANES, DECAY: 2 * PLANES}
    LN_G, LN_B, BN_G, BN_B, BN_MEAN, BN_VAR = (3 * PLANES + KT * j for j in range(6))
    B_DOWN = BN_VAR + KT
    VECS = B_DOWN + E
    UP1 = KT * 2 * P
    UP2 = UP1 + D
    HB = UP2 + D
    EXPERT = HB + 2

    x_t = x.rearrange("b (t p) d -> b p t d", p=P)
    out_t = out.rearrange("b (t p) d -> b p t d", p=P)
    comb_dram = nc.dram_tensor("comb_dram", [2, M * S], F32, kind="Internal").ap()

    with ExitStack() as ctx:
        def sb(name, shape, dt=F32):
            return ctx.enter_context(nc.sbuf_tensor(name, shape, dt))

        def sem(name):
            return ctx.enter_context(nc.semaphore(name))

        w_hi = sb("w_hi", [P, M * 3, KT, D], F16)
        w_lo = sb("w_lo", [P, M * 3, KT, D], F16)
        w_stage = sb("w_stage", [P, 2, 3, KT, D])
        gw_stage = sb("gw_stage", [P, KT, M])
        gw_hi = sb("gw_hi", [P, KT, M], F16)
        gw_lo = sb("gw_lo", [P, KT, M], F16)
        vec_rows = sb("vec_rows", [VECS, P])
        vecs = sb("vecs", [P, VECS])
        experts = sb("experts", [P, E, EXPERT], F16)
        expert = sb("expert", [P, EXPERT], F16)
        wr = sb("wr", [P, KT, E])
        br_all = sb("br_all", [P, E])
        ident = sb("ident", [P, P])
        ones = sb("ones", [P, P])
        neg_half = sb("neg_half", [P, T])
        rank_init = sb("rank_init", [P, T, M])
        order8 = sb("order8", [P, E])
        route_mul = sb("route_mul", [P, KT])
        route_add = sb("route_add", [P, KT])
        small = sb("small", [P, 8, KT])
        x_in = sb("x_in", [P, 2, T, D])
        resid = sb("resid", [P, T, D])
        normed = sb("normed", [P, T, D])
        xh = sb("xh", [P, 2, KT, S], F16)
        xl = sb("xl", [P, 2, KT, S], F16)
        u_split = sb("u_split", [P, 2, KT, S], F16)
        uh, ul = u_split[:, 0], u_split[:, 1]
        gate_s = sb("gate_s", [P, 2, S])
        value_s = sb("value_s", [P, 2, S])
        decay_s = sb("decay_s", [P, 2, S])
        hid = sb("hid", [P, 4, S])
        acc = sb("acc", [P, 2, KT, S])
        comb_all = sb("comb_all", [P, M, S])
        h32 = sb("h32", [P, S])
        up_in1 = sb("up_in1", [P, S], F16)
        up_in2 = sb("up_in2", [P, S], F16)
        down_stage = u_split[:].bitcast(F32).rearrange("p a k (e j) -> p (a k e) j", j=P).rearrange(
            "p (e k) j -> p e k j", k=KT)
        up_stage = resid[:]
        up_bias_stage = acc[:, 1].rearrange("p a (e j) -> p (a e) j", j=D)
        stats = {k: sb("stats_" + k, [P, T, 6]) for k in "xaty"}
        moments = {k: sb("moments_" + k, [P, 5, T]) for k in "xaty"}
        root_in = {k: sb("root_in_" + k, [P, T]) for k in "xaty"}
        root = {k: sb("root_" + k, [P, T]) for k in "xaty"}
        mul_by = {k: sb("mul_by_" + k, [P, T]) for k in "xty"}
        mean = {k: sb("mean_" + k, [P, T]) for k in "xt"}
        add_y = sb("add_y", [P, T])
        shift_a = sb("shift_a", [P, T])
        logit = sb("logit", [P, T, M])
        beats = sb("beats", [P, 6, T])
        rank = sb("rank", [P, T, M])
        chosen = sb("chosen", [P, T, M])
        chosen_logit = sb("chosen_logit", [P, T, M])
        pair_sum = sb("pair_sum", [P, T])
        margin = sb("margin", [P, T, M])
        share = sb("share", [P, T, M])
        comb = sb("comb", [P, M, T])
        comb_rows = sb("comb_rows", [M * T, P])
        u_sums = sb("u_sums", [P, KT, C])
        z_mean = sb("z_mean", [P, 3, KT])
        z_all = sb("z_all", [P, KT, P])
        r8 = sb("r8", [P, 8, E])
        r1 = sb("r1", [P, 8])
        index = sb("index", [P, 1], I32)

        ps_main = ctx.enter_context(nc.psum_tensor("ps_main", [P, BANKS, CHUNK], F32))
        ps_aux = ctx.enter_context(nc.psum_tensor("ps_aux", [P, 4, CHUNK], F32))
        ps_misc = ctx.enter_context(nc.psum_tensor("ps_misc", [P, CHUNK], F32))
        ps_gates = ps_misc[:, 0:T * M]
        ps_route = ps_misc[:, 64:64 + E]
        ps_comb = ps_misc[0:M * T, P:2 * P]
        ps_vecs = ps_misc[:, 0:VECS]
        ps_bias = ps_misc[:, 64:64 + E]
        ps_tok = ps_aux[:].rearrange("p b (a d) -> p (b a) d", a=2)

        vecs_loaded, gw_loaded, misc_loaded = sem("vecs_loaded"), sem("gw_loaded"), sem("misc_loaded")
        w_loaded = [sem(f"w_loaded{m}") for m in range(M)]
        experts_loaded = sem("experts_loaded")
        rows_zero, pool_consts = sem("rows_zero"), sem("pool_consts")
        consts, ident_zero, ident_ready = sem("consts"), sem("ident_zero"), sem("ident_ready")
        vecs_turned, vecs_ready = sem("vecs_turned"), sem("vecs_ready")
        w_hi_ready, w_lo_ready = sem("w_hi_ready"), sem("w_lo_ready")
        bn_root_in, bn_root, prep_link = sem("bn_root_in"), sem("bn_root"), sem("prep_link")
        bias_turned, experts_ready = sem("bias_turned"), sem("experts_ready")
        main_filled = sem("main_filled")
        main_read = sem("main_read")
        decay_ready = sem("decay_ready")
        input_ready = sem("input_ready")
        scanned = sem("scanned")
        weighed = sem("weighed")
        summed = sem("summed")
        x_loaded = sem("x_loaded")
        x_link = sem("x_link")
        x_root_in, x_root, x_scaled = sem("x_root_in"), sem("x_root"), sem("x_scaled")
        x_normed, x_turned = sem("x_normed"), sem("x_turned")
        xh_ready, xl_ready = sem("xh_ready"), sem("xl_ready")
        gates_done, mix_link, margin_ready = sem("gates_done"), sem("mix_link"), sem("margin_ready")
        share_ready, comb_ready, comb_turned = sem("share_ready"), sem("comb_ready"), sem("comb_turned")
        comb_copied, comb_saved = sem("comb_copied"), sem("comb_saved")
        comb_loaded = [sem(f"comb_loaded{m}") for m in range(M)]
        a_turned, a_link, a_root_in, a_root = sem("a_turned"), sem("a_link"), sem("a_root_in"), sem("a_root")
        t_free, t_ready, t_link = sem("t_free"), sem("t_ready"), sem("t_link")
        t_root_in, t_root, t_scaled, u_ready, u_turned = (
            sem("t_root_in"), sem("t_root"), sem("t_scaled"), sem("u_ready"), sem("u_turned"))
        uh_ready, ul_ready = sem("uh_ready"), sem("ul_ready")
        route_link, z_ready, route_done = sem("route_link"), sem("z_ready"), sem("route_done")
        delta_ready, sig_ready, index_ready = sem("delta_ready"), sem("sig_ready"), sem("index_ready")
        expert_loaded, down_done, h_ready = sem("expert_loaded"), sem("down_done"), sem("h_ready")
        hh_ready, up_in_ready, up_done = sem("hh_ready"), sem("up_in_ready"), sem("up_done")
        y_link, y_root_in, y_root = sem("y_link"), sem("y_root_in"), sem("y_root")
        index_seen = sem("index_seen")
        out_ready, out_stored = sem("out_ready"), sem("out_stored")

        MIX_LINKS, ROUTE_LINKS, STAT_LINKS, Y_LINKS = 11, 12, 4, 7

        def iterations(eng, run):
            def turn(j, r):
                return Batch(2 * j + r, r % 2)
            run(turn(0, 0), turn(0, 1), None)
            with eng.Fori(0, B // 2 - 1) as j:
                for r in (1, 2):
                    run(turn(j, r), turn(j, r + 1), turn(j, r - 1))
            run(turn(0, B - 1), None, turn(0, B - 2))
            run(None, None, turn(0, B - 1))

        def chunk(c):
            return slice(c * CHUNK, (c + 1) * CHUNK)

        def tile(t):
            return slice(t * P, (t + 1) * P)

        block = ctx.enter_context(nc.Block())

        @block.sync
        def _(sp):
            def load_mixer(m):
                for j, w in enumerate((Wg, Wd, Wv)):
                    sp.dma_start(w_stage[:, m % 2, j], w[m].rearrange("(k p) e -> p k e", p=P)
                                 ).then_inc(w_loaded[m], 16)

            def load_comb(nx, m):
                sp.dma_start(comb_all[:, m, :],
                             comb_dram[nx.par, m * S:(m + 1) * S].rearrange("(a s) -> a s", a=1)
                             .broadcast_to([P, S])).then_inc(comb_loaded[m], 16)

            def save_comb(nx):
                sp.wait_ge(comb_copied, nx.n + 1)
                sp.dma_start(comb_dram[nx.par].rearrange("(r p) -> r p", p=P), comb_rows[:]
                             ).then_inc(comb_saved, 16)
                sp.wait_ge(comb_saved, 16 * nx.n + 16)

            sp.sem_inc(t_free, 1)
            sp.dma_start(x_in[:, 0], x_t[0]).then_inc(x_loaded, 16)
            row = 0
            for v in (bg, bv, bd):
                sp.dma_start(vec_rows[row:row + PLANES, :], v.rearrange("m (k p) -> (m k) p", p=P)
                             ).then_inc(vecs_loaded, 16)
                row += PLANES
            for v in (ln_g, ln_b, bn_g, bn_b, bn_mean, bn_var):
                sp.dma_start(vec_rows[row:row + KT, :], v.rearrange("(k p) -> k p", p=P)
                             ).then_inc(vecs_loaded, 16)
                row += KT
            for a in range(2):
                sp.dma_start(vec_rows[row:row + E, a * H:(a + 1) * H], b_down).then_inc(vecs_loaded, 16)
            load_mixer(0)
            sp.dma_start(gw_stage[:], gate_W.rearrange("(k p) m -> p k m", p=P)).then_inc(gw_loaded, 16)
            load_mixer(1)
            sp.dma_start(wr[:], Wr.rearrange("(k p) e -> p k e", p=P)).then_inc(misc_loaded, 16)
            sp.dma_start(br_all[:], br.rearrange("(a e) -> a e", a=1).broadcast_to([P, E])).then_inc(misc_loaded, 16)
            for k in range(KT):
                for a in range(2):
                    sp.dma_start(down_stage[:, :, k, a * H:(a + 1) * H],
                                 W_down[:, k * P:(k + 1) * P, :].rearrange("e p h -> p e h")
                                 ).then_inc(experts_loaded, 16)
            for a in range(2):
                sp.dma_start(up_stage[a * H:(a + 1) * H], W_up.rearrange("e h d -> h e d")
                             ).then_inc(experts_loaded, 16)
            for row in (64, 96):
                sp.dma_start(up_bias_stage[row:row + 1], b_up.rearrange("(a e) d -> a e d", a=1)
                             ).then_inc(experts_loaded, 16)
            for m in (2, 3):
                sp.wait_ge(w_hi_ready, m - 1)
                sp.wait_ge(w_lo_ready, m - 1)
                load_mixer(m)
                if m == 2:
                    save_comb(Batch(0, 0))
                    for mm in range(M):
                        load_comb(Batch(0, 0), mm)

            def run(bt, nx, pv):
                if nx:
                    if pv:
                        sp.wait_ge(t_ready, pv.n + 1)
                    else:
                        sp.wait_ge(x_root_in, 1)
                    sp.dma_start(x_in[:, nx.par], x_t[bass.ds(nx.n, 1)].rearrange("a p t d -> p (a t) d")
                                 ).then_inc(x_loaded, 16)
                if pv:
                    sp.wait_ge(experts_ready, 6)
                    sp.wait_ge(index_ready, 2 * pv.n + 2)
                    sp.sem_inc(index_seen, 1)
                    e = sp.value_load(index[0:1, 0:1], min_val=0, max_val=E - 1)
                    sp.dma_start(expert[:].bitcast(I32),
                                 experts[:].bitcast(I32)[:, bass.ds(e, 1), :].rearrange("p a c -> p (a c)")
                                 ).then_inc(expert_loaded, 16)
                if nx:
                    save_comb(nx)
                    for m in range(M - 1):
                        sp.wait_ge(weighed, PLANES * bt.n + KT * (m + 1))
                        load_comb(nx, m)
                if pv:
                    sp.wait_ge(out_ready, pv.n + 1)
                    sp.dma_start(out_t[bass.ds(pv.n, 1)].rearrange("a p t d -> p (a t) d"), resid[:]
                                 ).then_inc(out_stored, 16)
                    sp.wait_ge(out_stored, 16 * pv.n + 16)
                    sp.sem_inc(t_free, 1)
                if nx:
                    sp.wait_ge(weighed, PLANES * bt.n + PLANES)
                    load_comb(nx, M - 1)

            iterations(sp, run)

        @block.gpsimd
        def _(pool):
            pool.memset(ident[:], 0.0).then_inc(ident_zero, 1)
            pool.wait_ge(ident_zero, 1)
            pool.affine_select(out=ident[:], in_=ident[:], compare_op=ALU.not_equal, fill=1.0, base=0,
                               pattern=[[-1, P]], channel_multiplier=1).then_inc(ident_ready, 1)
            pool.memset(neg_half[:], -0.5).then_inc(pool_consts, 1)
            pool.memset(ones[:], 1.0).then_inc(pool_consts, 1)
            for m in range(M):
                pool.memset(rank_init[:, :, m], float(M - 1 - m)).then_inc(pool_consts, 1)
            for e in range(E):
                pool.memset(order8[:, e:e + 1], float(E - e)).then_inc(pool_consts, 1)

            def power(key, ready, done, n):
                pool.wait_ge(ready, n + 1)
                pool.tensor_tensor(root[key][:], root_in[key][:], neg_half[:], ALU.pow).then_inc(done, 1)

            pool.wait_ge(pool_consts, 2 + M + E)
            power("x", x_root_in, x_root, 0)

            def bn_power():
                pool.wait_ge(bn_root_in, 1)
                pool.tensor_tensor(small[:, 1], small[:, 0], neg_half[:, 0:KT], ALU.pow).then_inc(bn_root, 1)

            def multiply(bt, p):
                pool.wait_ge(main_read, EVAC * bt.n + 6 * p + 6)
                pool.tensor_tensor(value_s[:, p % 2], gate_s[:, p % 2], value_s[:, p % 2], ALU.mult
                                   ).then_inc(input_ready, 1)

            def add(bt, p):
                pool.wait_ge(weighed, PLANES * bt.n + p + 1)
                if p >= 2 * KT:
                    pool.wait_ge(summed, ADDS * bt.n + p - 2 * KT + 1)
                a = acc[:, bt.par, p % KT]
                pool.tensor_tensor(a, a, hid[:, p % 4], ALU.add).then_inc(summed, 1)

            def run(bt, nx, pv):
                if pv:
                    add(pv, PLANES - 1)
                for p in range(PLANES):
                    if p == 1 and pv:
                        power("a", a_root_in, a_root, pv.n)
                    if p == 1 and not pv:
                        bn_power()
                    if p == 2 and pv:
                        power("t", t_root_in, t_root, pv.n)
                    if p == 3 and nx:
                        power("x", x_root_in, x_root, nx.n)
                    if p == 7 and bt:
                        add(bt, 6)
                    if bt:
                        multiply(bt, p)
                    if p == 6 and pv:
                        power("y", y_root_in, y_root, pv.n)
                    if p in (3, 4, 5, 6) and bt:
                        add(bt, p - 1)

            iterations(pool, run)

        @block.scalar
        def _(act):
            def mixer_high(m):
                act.wait_ge(w_loaded[m], 48)
                act.activation(w_hi[:, 3 * m:3 * m + 3], w_stage[:, m % 2], ACT.Copy, scale=W_SCALE
                               ).then_inc(w_hi_ready, 1)

            def high_x(nx):
                act.wait_ge(x_turned, nx.n + 1)
                for k in range(KT):
                    for c in range(C):
                        act.activation(xh[:, nx.par, k, chunk(c)], ps_aux[:, C * k + c], ACT.Copy
                                       ).then_inc(xh_ready, 1)

            def shares(nx):
                act.wait_ge(margin_ready, nx.n + 1)
                act.activation(share[:], margin[:], ACT.Sigmoid).then_inc(share_ready, 1)

            def evacuate(bt, p, kind, first):
                m, half = divmod(p, KT)
                col = BIAS[kind] + KT * m + half
                if kind == GATE and not (first and p < 2):
                    act.wait_ge(input_ready, PLANES * bt.n + p - 1)
                if kind == DECAY and not (first and p < 2):
                    act.wait_ge(scanned, PLANES * bt.n + p - 1)
                buf = {GATE: gate_s, DECAY: decay_s, VALUE: value_s}[kind]
                for c in range(C):
                    n = 6 * p + 2 * kind + c
                    act.wait_ge(main_filled, EVAC * bt.n + n + 1)
                    act.activation(buf[:, p % 2, chunk(c)], ps_main[:, n % BANKS],
                                   ACT.Tanh if kind == VALUE else ACT.Sigmoid,
                                   bias=vecs[:, col:col + 1], scale=Q_W).then_inc(main_read, 1)
                if kind == VALUE:
                    act.wait_ge(main_read, EVAC * bt.n + 6 * p + 4)
                    act.activation(decay_s[:, p % 2], decay_s[:, p % 2], ACT.Copy, bias=0.001, scale=0.998
                                   ).then_inc(decay_ready, 1)

            def high_u(pv):
                act.wait_ge(u_turned, pv.n + 1)
                for k in range(KT):
                    for c in range(C):
                        act.activation(uh[:, k, chunk(c)], ps_aux[:, C * k + c], ACT.Copy,
                                       accum_out=u_sums[:, k, c:c + 1]).then_inc(uh_ready, 1)

            def router_sigmoids(pv):
                act.wait_ge(delta_ready, pv.n + 1)
                act.activation(r8[:, 1], r8[:, 0], ACT.Sigmoid)
                act.activation(r8[:, 2], r8[:, 0], ACT.Sigmoid, scale=-1.0).then_inc(sig_ready, 1)

            def hidden(pv):
                act.wait_ge(down_done, pv.n + 1)
                for c in range(C):
                    act.activation(h32[:, chunk(c)], ps_aux[:, c], ACT.Relu,
                                   bias=expert[:, HB:HB + 2].bitcast(F32), scale=Q_W * H_SCALE
                                   ).then_inc(h_ready, 1)
                for c in range(C):
                    act.wait_ge(h_ready, C * pv.n + c + 1)
                    act.activation(up_in1[:, chunk(c)], h32[:, chunk(c)], ACT.Copy).then_inc(hh_ready, 1)

            act.wait_ge(pool_consts, 2 + M + E)
            act.activation(share[:, 0, 0:1], ones[:, 0:1], ACT.Sigmoid)
            mixer_high(0)
            act.wait_ge(gw_loaded, 16)
            act.activation(gw_hi[:], gw_stage[:], ACT.Copy, scale=W_SCALE).then_inc(w_hi_ready, 1)
            high_x(Batch(0, 0))
            mixer_high(1)
            act.wait_ge(vecs_ready, 1)

            def run(bt, nx, pv):
                for s in range(STEPS):
                    p, kind = divmod(s, 3)
                    if pv:
                        if s == 11:
                            high_u(pv)
                        if s == 14:
                            router_sigmoids(pv)
                        if s == 18:
                            hidden(pv)
                    elif s == 2:
                        shares(bt)
                    elif s in (4, 8):
                        mixer_high(2 + (s == 8))
                    if nx:
                        if s == 15:
                            high_x(nx)
                        if s == 19:
                            shares(nx)
                    if bt:
                        evacuate(bt, p, kind, pv is None)

            iterations(act, run)

        @block.vector
        def _(dve):
            def linker(sem_, base):
                count = [0]

                def link(ins):
                    count[0] += 1
                    ins.then_inc(sem_, 1)
                    dve.wait_ge(sem_, base + count[0])
                link.count = count
                return link

            def moments_of(key, rows, link):
                for t in range(T):
                    ins = dve.bn_stats(out=stats[key][:, t], in_=rows(t))
                link(ins)
                even, odd = stats[key][:, :, 0:3], stats[key][:, :, 3:6]
                mom = moments[key]
                dve.tensor_tensor(mom[:, 0], even[:, :, 1], odd[:, :, 1], ALU.add)
                dve.tensor_tensor(mom[:, 1], even[:, :, 2], odd[:, :, 2], ALU.add)
                link(dve.tensor_tensor(mom[:, 2], even[:, :, 1], odd[:, :, 1], ALU.subtract))
                link(dve.tensor_tensor(mom[:, 3], mom[:, 2], mom[:, 2], ALU.mult))
                link(dve.scalar_tensor_tensor(mom[:, 4], mom[:, 3], D / 4, mom[:, 1], ALU.mult, ALU.add))

            def mixer_low(m):
                dve.wait_ge(w_hi_ready, m + 1 + (m > 0))
                dve.scalar_tensor_tensor(w_lo[:, 3 * m:3 * m + 3].rearrange("p a k e -> p (a k e)"),
                                         w_stage[:, m % 2].rearrange("p a k e -> p (a k e)"), W_SCALE,
                                         w_hi[:, 3 * m:3 * m + 3].rearrange("p a k e -> p (a k e)"),
                                         ALU.mult, ALU.subtract).then_inc(w_lo_ready, 1)

            def x_moments(nx):
                dve.wait_ge(x_loaded, 16 * nx.n + 16)
                link = linker(x_link, STAT_LINKS * nx.n)
                moments_of("x", lambda t: x_in[:, nx.par, t], link)
                assert link.count[0] == STAT_LINKS
                dve.tensor_scalar(root_in["x"][:], moments["x"][:, 4], 1 / D, EPS, ALU.mult, ALU.add
                                  ).then_inc(x_root_in, 1)

            def normalise(key, rows, root_ready, scaled, b, done):
                dve.wait_ge(root_ready, b.n + 1)
                dve.tensor_scalar(mul_by[key][:], root[key][:], X_SCALE, None, ALU.mult)
                dve.tensor_scalar(mean[key][:], moments[key][:, 0], 0.5, None, ALU.mult).then_inc(scaled, 1)
                dve.wait_ge(scaled, b.n + 1)
                for t in range(T):
                    ins = dve.tensor_scalar(normed[:, t], rows[:, t], mean[key][:, t:t + 1],
                                            mul_by[key][:, t:t + 1], ALU.subtract, ALU.mult)
                ins.then_inc(done, 1)

            def low_x(nx):
                for k in range(KT):
                    for c in range(C):
                        dve.wait_ge(xh_ready, KT * C * nx.n + C * k + c + 1)
                        dve.tensor_tensor(xl[:, nx.par, k, chunk(c)], ps_aux[:, C * k + c],
                                          xh[:, nx.par, k, chunk(c)], ALU.subtract).then_inc(xl_ready, 1)

            def rank_mixers(nx):
                link = linker(mix_link, MIX_LINKS * nx.n)
                dve.wait_ge(gates_done, nx.n + 1)
                link(dve.tensor_scalar(logit[:], ps_gates.rearrange("p (t m) -> p t m", m=M), Q_W, None, ALU.mult))
                b = beats[:].rearrange("p c t -> p t c")
                at = 0
                parts = []
                for d in range(1, M):
                    n = M - d
                    ins = dve.tensor_tensor(b[:, :, at:at + n], logit[:, :, 0:n], logit[:, :, d:M], ALU.is_ge)
                    parts.append((d, n, at))
                    at += n
                link(ins)
                src = rank_init
                for d, n, at in parts:
                    if d == 1:
                        dve.tensor_copy(rank[:, :, M - 1:M], rank_init[:, :, M - 1:M])
                    link(dve.tensor_tensor(rank[:, :, 0:n], src[:, :, 0:n], b[:, :, at:at + n], ALU.subtract))
                    link(dve.tensor_tensor(rank[:, :, d:M], rank[:, :, d:M], b[:, :, at:at + n], ALU.add))
                    src = rank
                link(dve.tensor_scalar(chosen[:], rank[:], 1.5, None, ALU.is_lt))
                link(dve.tensor_tensor(chosen_logit[:], chosen[:], logit[:], ALU.mult))
                link(dve.tensor_reduce(pair_sum[:], chosen_logit[:], AX.X, ALU.add))
                dve.scalar_tensor_tensor(margin[:], logit[:], 2.0, pair_sum[:].broadcast_to([P, T, M]),
                                         ALU.mult, ALU.subtract).then_inc(margin_ready, 1)
                return link

            def weights_of(nx):
                dve.wait_ge(share_ready, nx.n + 1)
                dve.tensor_tensor(comb[:].rearrange("p m t -> p t m"), share[:], chosen[:], ALU.mult
                                  ).then_inc(comb_ready, 1)

            def copy_weights(nx, first):
                dve.wait_ge(comb_turned, nx.n + 1)
                if not first:
                    dve.wait_ge(comb_saved, 16 * nx.n)
                dve.tensor_copy(comb_rows[:], ps_comb).then_inc(comb_copied, 1)

            def scan(bt, p, first):
                dve.wait_ge(decay_ready, PLANES * bt.n + p + 1)
                dve.wait_ge(input_ready, PLANES * bt.n + p + 1)
                if p >= 2 * KT + 2:
                    dve.wait_ge(summed, ADDS * bt.n + p - 5)
                elif p < 4 and not first:
                    dve.wait_ge(summed, ADDS * bt.n + p - 3)
                dve.tensor_tensor_scan(hid[:, p % 4], decay_s[:, p % 2], value_s[:, p % 2], 0.0,
                                       ALU.mult, ALU.add).then_inc(scanned, 1)

            def weigh(bt, p):
                m, half = divmod(p, KT)
                dve.wait_ge(scanned, PLANES * bt.n + p + 1)
                if half == 0:
                    dve.wait_ge(comb_loaded[m], 16 * bt.n + 16)
                dst = acc[:, bt.par, half] if m == 0 else hid[:, p % 4]
                dve.tensor_tensor(dst, hid[:, p % 4], comb_all[:, m], ALU.mult).then_inc(weighed, 1)

            def a_moments(pv):
                dve.wait_ge(a_turned, pv.n + 1)
                link = linker(a_link, STAT_LINKS * pv.n)
                moments_of("a", lambda t: ps_tok[:, t], link)
                dve.tensor_scalar(root_in["a"][:], moments["a"][:, 4], 1 / D, EPS, ALU.mult, ALU.add
                                  ).then_inc(a_root_in, 1)

            def residual(pv):
                dve.wait_ge(a_root, pv.n + 1)
                dve.wait_ge(t_free, pv.n + 1)
                dve.scalar_tensor_tensor(shift_a[:], moments["a"][:, 0], 0.5, root["a"][:], ALU.mult, ALU.mult)
                for t in range(T):
                    ins = dve.scalar_tensor_tensor(resid[:, t], ps_tok[:, t], root["a"][:, t:t + 1],
                                                   x_in[:, pv.par, t], ALU.mult, ALU.add)
                ins.then_inc(t_ready, 1)

            def t_moments(pv):
                link = linker(t_link, STAT_LINKS * pv.n)
                dve.wait_ge(t_ready, pv.n + 1)
                moments_of("t", lambda t: resid[:, t], link)
                dve.tensor_scalar(root_in["t"][:], moments["t"][:, 4], (1.0 + EPS) / D, EPS * EPS, ALU.mult, ALU.add
                                  ).then_inc(t_root_in, 1)

            def low_u(pv):
                for k in range(KT):
                    for c in range(C):
                        dve.wait_ge(uh_ready, KT * C * pv.n + C * k + c + 1)
                        dve.tensor_tensor(ul[:, k, chunk(c)], ps_aux[:, C * k + c], uh[:, k, chunk(c)],
                                          ALU.subtract).then_inc(ul_ready, 1)

            def route_in(pv):
                link = linker(route_link, ROUTE_LINKS * pv.n)
                dve.wait_ge(uh_ready, KT * C * (pv.n + 1))
                link(dve.tensor_tensor(z_mean[:, 0], u_sums[:, :, 0], u_sums[:, :, 1], ALU.add))
                link(dve.tensor_tensor(z_mean[:, 1], z_mean[:, 0], route_mul[:], ALU.mult))
                link(dve.tensor_tensor(z_mean[:, 2], z_mean[:, 1], route_add[:], ALU.add))
                for k in range(KT):
                    ins = dve.tensor_scalar(z_all[:, k], ones[:], z_mean[:, 2, k:k + 1], None, ALU.mult)
                ins.then_inc(z_ready, 1)

            def route_logits(pv):
                link = linker(route_link, ROUTE_LINKS * pv.n + 3)
                dve.wait_ge(route_done, pv.n + 1)
                link(dve.tensor_tensor(r8[:, 3], ps_route, br_all[:], ALU.add))
                link(dve.tensor_reduce(r1[:, 0:1], r8[:, 3], AX.X, ALU.max))
                dve.tensor_scalar(r8[:, 0], r8[:, 3], r1[:, 0:1], None, ALU.subtract).then_inc(delta_ready, 1)

            def route_pick(pv):
                link = linker(route_link, ROUTE_LINKS * pv.n + 5)
                dve.wait_ge(sig_ready, pv.n + 1)
                link(dve.reciprocal(r8[:, 4], r8[:, 2]))
                link(dve.tensor_tensor(r8[:, 5], r8[:, 4], r8[:, 1], ALU.mult))
                link(dve.tensor_reduce(r1[:, 1:2], r8[:, 5], AX.X, ALU.add))
                link(dve.reciprocal(r1[:, 2:3], r1[:, 1:2]))
                link(dve.tensor_scalar(r8[:, 6], r8[:, 5], r1[:, 2:3], None, ALU.mult))
                link(dve.tensor_reduce(r1[:, 3:4], r8[:, 6], AX.X, ALU.max))
                link(dve.scalar_tensor_tensor(r8[:, 7], r8[:, 6], r1[:, 3:4], order8[:], ALU.is_equal, ALU.mult))
                dve.tensor_reduce(r1[:, 4:5], r8[:, 7], AX.X, ALU.max).then_inc(index_ready, 1)
                dve.wait_ge(index_ready, 2 * pv.n + 1)
                dve.tensor_scalar(index[:], r1[:, 4:5], -1.0, float(E), ALU.mult, ALU.add).then_inc(index_ready, 1)
                dve.tensor_scalar(r1[:, 5:6], r1[:, 3:4], 1 / (H_SCALE * W_SCALE), None, ALU.mult)
                return link

            def low_h(pv):
                dve.wait_ge(hh_ready, C * pv.n + C)
                dve.tensor_copy(up_in2[0:H, :], up_in1[0:H, :])
                dve.tensor_tensor(up_in1[H:P, :], h32[H:P, :], up_in1[H:P, :], ALU.subtract
                                  ).then_inc(up_in_ready, 1)

            def y_moments(pv):
                link = linker(y_link, Y_LINKS * pv.n)
                dve.wait_ge(up_done, pv.n + 1)
                dve.scalar_tensor_tensor(r1[:, 6:7], r1[:, 5:6], 1 / D, r1[:, 5:6], ALU.mult, ALU.mult)
                moments_of("y", lambda t: ps_tok[:, t], link)
                dve.tensor_scalar(root_in["y"][:], moments["y"][:, 4], r1[:, 6:7], EPS, ALU.mult, ALU.add
                                  ).then_inc(y_root_in, 1)

            def finish(pv):
                link = linker(y_link, Y_LINKS * pv.n + STAT_LINKS)
                dve.wait_ge(y_root, pv.n + 1)
                link(dve.tensor_scalar(mul_by["y"][:], root["y"][:], r1[:, 5:6], None, ALU.mult))
                dve.scalar_tensor_tensor(add_y[:], moments["y"][:, 0], 0.5, mul_by["y"][:], ALU.mult, ALU.mult)
                for t in range(T):
                    ins = dve.scalar_tensor_tensor(resid[:, t], ps_tok[:, t], mul_by["y"][:, t:t + 1],
                                                   resid[:, t], ALU.mult, ALU.add)
                link(ins)
                link(dve.tensor_tensor(add_y[:], add_y[:], shift_a[:], ALU.add))
                for t in range(T):
                    ins = dve.tensor_scalar(resid[:, t], resid[:, t], add_y[:, t:t + 1], None, ALU.subtract)
                ins.then_inc(out_ready, 1)

            first = Batch(0, 0)
            dve.memset(up_in2[H:P, :], 0.0)
            dve.memset(experts[H:P, :, UP2:HB], 0.0).then_inc(rows_zero, 1)
            dve.wait_ge(rows_zero, 1)
            for row in (64, 96):
                dve.memset(up_in2[row:row + 1, :], H_SCALE).then_inc(consts, 1)
            x_moments(first)
            mixer_low(0)
            normalise("x", x_in[:, 0], x_root, x_scaled, first, x_normed)
            dve.wait_ge(w_hi_ready, 2)
            dve.scalar_tensor_tensor(gw_lo[:], gw_stage[:], W_SCALE, gw_hi[:], ALU.mult, ALU.subtract
                                     ).then_inc(consts, 1)
            dve.wait_ge(vecs_turned, 1)
            dve.tensor_copy(vecs[:], ps_vecs).then_inc(vecs_ready, 1)
            low_x(first)
            dve.wait_ge(pool_consts, 2 + M + E)

            def prepare_router():
                link = linker(prep_link, 0)
                dve.wait_ge(vecs_ready, 1)
                v = {k: vecs[:, c:c + KT] for k, c in (("g", LN_G), ("b", LN_B), ("bg", BN_G), ("bb", BN_B),
                                                       ("mean", BN_MEAN), ("var", BN_VAR))}
                dve.tensor_scalar(small[:, 0], v["var"], EPS, None, ALU.add).then_inc(bn_root_in, 1)
                dve.wait_ge(bn_root, 1)
                link(dve.tensor_tensor(small[:, 2], small[:, 1], v["bg"], ALU.mult))
                link(dve.tensor_tensor(small[:, 3], v["b"], v["mean"], ALU.subtract))
                link(dve.tensor_tensor(small[:, 4], small[:, 3], small[:, 2], ALU.mult))
                link(dve.tensor_tensor(route_add[:], small[:, 4], v["bb"], ALU.add))
                link(dve.scalar_tensor_tensor(route_mul[:], small[:, 2], 1 / (X_SCALE * S), v["g"], ALU.mult, ALU.mult))
                return link

            def prepare_experts(link):
                dve.wait_ge(experts_loaded, 16 * 8)
                link(dve.tensor_scalar(small[:, 5], vecs[:, LN_G:LN_G + KT], W_SCALE, None, ALU.mult))
                for k in range(KT):
                    hi = experts[:, :, (2 * k) * P:(2 * k + 1) * P]
                    lo = experts[:, :, (2 * k + 1) * P:(2 * k + 2) * P]
                    link(dve.tensor_scalar(hi, down_stage[:, :, k], small[:, 5, k:k + 1], None, ALU.mult))
                    dve.scalar_tensor_tensor(lo, down_stage[:, :, k], small[:, 5, k:k + 1], hi,
                                             ALU.mult, ALU.subtract).then_inc(experts_ready, 1)
                up1 = experts[:, :, UP1:UP2]
                up2 = experts[:, :, UP2:HB]
                link(dve.tensor_scalar(up1, up_stage, W_SCALE, None, ALU.mult))
                dve.scalar_tensor_tensor(up2[0:H], up_stage[0:H], W_SCALE, up1[0:H], ALU.mult, ALU.subtract
                                         ).then_inc(experts_ready, 1)
                for row in (64, 96):
                    r = slice(row, row + 1)
                    ins = dve.tensor_scalar(up2[r], up_bias_stage[r], W_SCALE, None, ALU.mult)
                    if row == 64:
                        ins.then_inc(experts_ready, 1)
                link(ins)
                dve.scalar_tensor_tensor(up2[r], up_bias_stage[r], W_SCALE, up2[r], ALU.mult, ALU.subtract
                                         ).then_inc(experts_ready, 1)
                dve.wait_ge(bias_turned, 1)
                link(dve.tensor_tensor(r8[:, 0], ps_bias, vecs[:, B_DOWN:B_DOWN + E], ALU.add))
                dve.tensor_scalar(experts[:, :, HB:HB + 2].bitcast(F32).rearrange("p e a -> p (e a)"), r8[:, 0],
                                  H_SCALE, None, ALU.mult).then_inc(experts_ready, 1)

            def run(bt, nx, pv):
                def plane(b, p):
                    if b:
                        scan(b, p, pv is None)
                        weigh(b, p)

                if pv:
                    plane(pv, PLANES - 1)
                    a_moments(pv)
                else:
                    mixer_low(1)
                    rank_mixers(bt)
                    weights_of(bt)
                    copy_weights(bt, True)
                    mixer_low(2)
                    prep = prepare_router()
                plane(bt, 0)
                if pv:
                    residual(pv)
                    t_moments(pv)
                else:
                    mixer_low(3)
                plane(bt, 1)
                if pv:
                    normalise("t", resid, t_root, t_scaled, pv, u_ready)
                else:
                    prepare_experts(prep)
                plane(bt, 2)
                if nx:
                    x_moments(nx)
                if pv:
                    route_in(pv)
                    low_u(pv)
                if nx:
                    if pv:
                        dve.wait_ge(u_turned, pv.n + 1)
                    else:
                        dve.wait_ge(x_turned, 1)
                    normalise("x", x_in[:, nx.par], x_root, x_scaled, nx, x_normed)
                if pv:
                    route_logits(pv)
                plane(bt, 3)
                if pv:
                    route_pick(pv)
                if nx:
                    low_x(nx)
                plane(bt, 4)
                if nx:
                    rank_mixers(nx)
                if pv:
                    low_h(pv)
                plane(bt, 5)
                if nx:
                    weights_of(nx)
                if pv:
                    y_moments(pv)
                if nx:
                    copy_weights(nx, False)
                plane(bt, 6)
                if pv:
                    finish(pv)

            iterations(dve, run)

        @block.tensor
        def _(pe):
            def turn_rows(rows_of, done):
                for k in range(KT):
                    for t in range(T):
                        ins = pe.transpose(ps_aux[:, C * k + t // 4, tile(t % 4)],
                                           normed[:, t, k * P:(k + 1) * P], ident[:])
                ins.then_inc(done, 1)

            def turn_x(nx):
                pe.wait_ge(x_normed, nx.n + 1)
                turn_rows(normed, x_turned)

            def gates(nx):
                pe.wait_ge(xh_ready, KT * C * (nx.n + 1))
                pe.wait_ge(xl_ready, KT * C * (nx.n + 1))
                for t in range(T):
                    n = 0
                    for k in range(KT):
                        for a, b in ((xh, gw_hi), (xh, gw_lo), (xl, gw_hi)):
                            ins = pe.matmul(ps_gates[:, M * t:M * (t + 1)], a[:, nx.par, k, tile(t)], b[:, k],
                                            start=(n == 0), stop=(n == 3 * KT - 1))
                            n += 1
                ins.then_inc(gates_done, 1)

            def turn_weights(nx):
                pe.wait_ge(comb_ready, nx.n + 1)
                pe.transpose(ps_comb, comb[:].rearrange("p m t -> p (m t)"), ident[:]).then_inc(comb_turned, 1)

            def product(bt, p, kind, first):
                m, half = divmod(p, KT)
                if kind == GATE and p == 0:
                    pe.wait_ge(xh_ready, KT * C * (bt.n + 1))
                    pe.wait_ge(xl_ready, KT * C * (bt.n + 1))
                if first and kind == GATE and half == 0:
                    pe.wait_ge(w_hi_ready, m + 1 + (m > 0))
                    pe.wait_ge(w_lo_ready, m + 1)
                for c in range(C):
                    n = 6 * p + 2 * kind + c
                    if not (first and n < BANKS):
                        pe.wait_ge(main_read, EVAC * bt.n + n - BANKS + 1)
                    i = 0
                    for k in range(KT):
                        for w, v in ((w_hi, xh), (w_lo, xh), (w_hi, xl)):
                            ins = pe.matmul(ps_main[:, n % BANKS], w[:, 3 * m + kind, k, half * P:(half + 1) * P],
                                            v[:, bt.par, k, chunk(c)], start=(i == 0), stop=(i == 3 * KT - 1))
                            i += 1
                    ins.then_inc(main_filled, 1)

            def turn_a(pv):
                pe.wait_ge(summed, ADDS * pv.n + ADDS)
                for t in range(T):
                    for k in range(KT):
                        ins = pe.transpose(ps_tok[:, t, k * P:(k + 1) * P], acc[:, pv.par, k, tile(t)], ident[:])
                ins.then_inc(a_turned, 1)

            def turn_u(pv):
                pe.wait_ge(u_ready, pv.n + 1)
                turn_rows(normed, u_turned)

            def route(pv):
                pe.wait_ge(z_ready, pv.n + 1)
                for k in range(KT):
                    ins = pe.matmul(ps_route, z_all[:, k], wr[:, k], start=(k == 0), stop=(k == KT - 1))
                ins.then_inc(route_done, 1)

            def down(pv):
                pe.wait_ge(expert_loaded, 16 * pv.n + 16)
                pe.wait_ge(ul_ready, KT * C * (pv.n + 1))
                for c in range(C):
                    i = 0
                    for k in range(KT):
                        for part, v in ((0, uh), (1, uh), (0, ul)):
                            ins = pe.matmul(ps_aux[:, c], expert[:, (2 * k + part) * P:(2 * k + part + 1) * P],
                                            v[:, k, chunk(c)], start=(i == 0), stop=(i == 3 * KT - 1))
                            i += 1
                ins.then_inc(down_done, 1)

            def up(pv):
                pe.wait_ge(up_in_ready, pv.n + 1)
                for t in range(T):
                    pe.matmul(ps_tok[:, t], up_in1[:, tile(t)], expert[:, UP1:UP2], start=True, stop=False)
                    ins = pe.matmul(ps_tok[:, t], up_in2[:, tile(t)], expert[:, UP2:HB], start=False, stop=True)
                ins.then_inc(up_done, 1)

            first = Batch(0, 0)
            pe.wait_ge(ident_ready, 1)
            pe.wait_ge(vecs_loaded, 16 * 11)
            pe.transpose(ps_vecs, vec_rows[:], ident[0:VECS, 0:VECS]).then_inc(vecs_turned, 1)
            turn_x(first)
            pe.wait_ge(vecs_ready, 1)
            pe.wait_ge(consts, 3)

            def hidden_bias():
                pe.wait_ge(experts_loaded, 16 * 8)
                pe.wait_ge(misc_loaded, 32)
                pe.wait_ge(comb_copied, 1)
                for e in range(E):
                    for k in range(KT):
                        ins = pe.matmul(ps_bias[:, e:e + 1], down_stage[:, e, k], vecs[:, LN_B + k:LN_B + k + 1],
                                        start=(k == 0), stop=(k == KT - 1))
                ins.then_inc(bias_turned, 1)

            def run(bt, nx, pv):
                for s in range(STEPS):
                    p, kind = divmod(s, 3)
                    if not pv:
                        if s == 1:
                            gates(bt)
                        if s == 4:
                            turn_weights(bt)
                        if s == 6:
                            hidden_bias()
                    if pv and s == 4:
                        turn_a(pv)
                    if pv and s == 11:
                        turn_u(pv)
                    if pv and s == 13:
                        route(pv)
                    if nx and s == 15:
                        if pv:
                            pe.wait_ge(ul_ready, KT * C * (pv.n + 1))
                        turn_x(nx)
                    if nx and s == 17:
                        gates(nx)
                    if pv and s == 17:
                        down(pv)
                    if pv and s == 20:
                        up(pv)
                    if nx and s == 21:
                        turn_weights(nx)
                    if bt:
                        product(bt, p, kind, pv is None)

            iterations(pe, run)


_INS = ["L0_attn_x", "L0_attn_Wg", "L0_attn_bg", "L0_attn_Wv", "L0_attn_bv", "L0_attn_Wd", "L0_attn_bd",
        "L0_attn_gate_W", "L0_ffn_ln_g", "L0_ffn_ln_b", "L0_ffn_bn_g", "L0_ffn_bn_b", "L0_ffn_bn_mean",
        "L0_ffn_bn_var", "L0_ffn_Wr", "L0_ffn_br", "L0_ffn_W_down", "L0_ffn_b_down", "L0_ffn_W_up",
        "L0_ffn_b_up"]


def kernel(**inputs):
    import numpy as np
    import concourse.bacc as bacc
    from concourse.bass_utils import run_bass_kernel_spmd

    nc = bacc.Bacc("TRN2", target_bir_lowering=False, num_devices=1)
    arrays, args = {}, []
    for name in _INS:
        a = np.ascontiguousarray(inputs[name])
        arrays[f"in_{name}"] = a
        args.append(nc.dram_tensor(f"in_{name}", a.shape, mybir.dt.from_np(a.dtype), kind="ExternalInput").ap())
    shape = inputs["L0_attn_x"].shape
    args.append(nc.dram_tensor("out", shape, F32, kind="ExternalOutput").ap())
    mixer_kernel(nc, *args)
    r = run_bass_kernel_spmd(nc, [arrays], core_ids=[0])
    return r.results[0]["out"]
```

```python
from collections import namedtuple
from contextlib import ExitStack

import concourse.bass as bass
from concourse import mybir

ALU = mybir.AluOpType
ACT = mybir.ActivationFunctionType
AX = mybir.AxisListType
F32 = mybir.dt.float32
F16 = mybir.dt.float16
I32 = mybir.dt.int32

P = 128
EPS = 1e-5
X_SCALE = 2.0 ** 11
W_SCALE = 2.0 ** 8
H_SCALE = 2.0 ** 6
Q_W = 1 / (X_SCALE * W_SCALE)
GATE, DECAY, VALUE = range(3)
KINDS = (GATE, DECAY, VALUE)
BANKS = 3
CHUNK = 512

Batch = namedtuple("Batch", "n par cut")
Piece = namedtuple("Piece", "q plane c")


def mixer_kernel(nc, x, Wg, bg, Wv, bv, Wd, bd, gate_W, ln_g, ln_b, bn_g, bn_b, bn_mean, bn_var,
                 Wr, br, W_down, b_down, W_up, b_up, out):
    B, S, D = x.shape
    M = Wg.shape[0]
    E, _, H = W_down.shape
    KT = D // P
    T = S // P
    C = S // CHUNK
    PLANES = M * KT
    EVAC = PLANES * 3 * C
    ADDS = PLANES - KT
    assert KT == 2 and T == 8 and C == 2 and M == 4 and 2 * H == P and EVAC % BANKS == 0
    assert B % 2 == 0 and B >= 4

    BIAS = {GATE: 0, VALUE: PLANES, DECAY: 2 * PLANES}
    LN_G, LN_B, BN_G, BN_B, BN_MEAN, BN_VAR = (3 * PLANES + KT * j for j in range(6))
    B_DOWN = BN_VAR + KT
    VECS = B_DOWN + E
    UP1 = KT * 2 * H
    UP2 = UP1 + D
    HB = UP2 + D
    EXPERT = HB + 2

    x_t = x.rearrange("b (t p) d -> b p t d", p=P)
    out_t = out.rearrange("b (t p) d -> b p t d", p=P)
    comb_dram = nc.dram_tensor("comb_dram", [2, M * S], F32, kind="Internal").ap()

    with ExitStack() as ctx:
        def sb(name, shape, dt=F32):
            return ctx.enter_context(nc.sbuf_tensor(name, shape, dt))

        def sem(name):
            return ctx.enter_context(nc.semaphore(name))

        w_hi = sb("w_hi", [P, M * 3, KT, D], F16)
        w_lo = sb("w_lo", [P, M * 3, KT, D], F16)
        w_stage = sb("w_stage", [P, 2, 3, KT, D])
        gw_stage = sb("gw_stage", [P, KT, M])
        gw = sb("gw", [P, KT, 2, M], F16)
        vec_rows = sb("vec_rows", [VECS, P])
        vecs = sb("vecs", [P, VECS])
        experts = sb("experts", [P, E, EXPERT], F16)
        expert = sb("expert", [P, EXPERT], F16)
        wr = sb("wr", [P, KT, E])
        br_all = sb("br_all", [P, E])
        ident = sb("ident", [P, P])
        ones = sb("ones", [P, P])
        neg_half = sb("neg_half", [P, T])
        rank_init = sb("rank_init", [P, T, M])
        order8 = sb("order8", [P, E])
        route_mul = sb("route_mul", [P, KT])
        route_add = sb("route_add", [P, KT])
        small = sb("small", [P, 8, KT])
        x_in = sb("x_in", [P, 2, T, D])
        resid = sb("resid", [P, T, D])
        normed = sb("normed", [P, T, D])
        xh = sb("xh", [P, 2, KT, S], F16)
        xl = sb("xl", [P, 2, KT, S], F16)
        u_split = sb("u_split", [P, 2, KT, S], F16)
        uh, ul = u_split[:, 0], u_split[:, 1]
        gate_s = sb("gate_s", [P, 2, S])
        value_s = sb("value_s", [P, 2, S])
        decay_s = sb("decay_s", [P, 2, S])
        hid = sb("hid", [P, 4, S])
        acc = sb("acc", [P, 2, KT, S])
        comb_all = sb("comb_all", [P, M, S])
        carry = sb("carry", [P, PLANES])
        h32 = sb("h32", [P, S])
        up_in1 = sb("up_in1", [P, S], F16)
        up_in2 = sb("up_in2", [P, S], F16)
        down_stage = u_split[:].bitcast(F32).rearrange("p a k (e j) -> p (a k e) j", j=P).rearrange(
            "p (e k) j -> p e k j", k=KT)
        up_stage = resid[:]
        up_bias_stage = acc[:, 1].rearrange("p a (e j) -> p (a e) j", j=D)
        stats = {k: sb("stats_" + k, [P, T, 6]) for k in "xaty"}
        moments = {k: sb("moments_" + k, [P, 5, T]) for k in "xaty"}
        root_in = {k: sb("root_in_" + k, [P, T]) for k in "xaty"}
        root = {k: sb("root_" + k, [P, T]) for k in "xaty"}
        mul_by = {k: sb("mul_by_" + k, [P, T]) for k in "xty"}
        mean = {k: sb("mean_" + k, [P, T]) for k in "xt"}
        shift_t = sb("shift_t", [P, T])
        add_y = sb("add_y", [P, T])
        shift_a = sb("shift_a", [P, T])
        logit = sb("logit", [P, T, M])
        beats = sb("beats", [P, 6, T])
        rank = sb("rank", [P, T, M])
        chosen = sb("chosen", [P, T, M])
        chosen_logit = sb("chosen_logit", [P, T, M])
        pair_sum = sb("pair_sum", [P, T])
        margin = sb("margin", [P, T, M])
        share = sb("share", [P, T, M])
        comb = sb("comb", [P, M, T])
        comb_rows = sb("comb_rows", [M * T, P])
        u_sums = sb("u_sums", [P, KT, C])
        z_mean = sb("z_mean", [P, 3, KT])
        z_wr = sb("z_wr", [P, 2, E])
        r8 = sb("r8", [P, 8, E])
        r1 = sb("r1", [P, 8])
        index = sb("index", [P, 1], I32)

        ps_main = ctx.enter_context(nc.psum_tensor("ps_main", [P, BANKS, CHUNK], F32))
        ps_aux = ctx.enter_context(nc.psum_tensor("ps_aux", [P, 4, CHUNK], F32))
        ps_misc = ctx.enter_context(nc.psum_tensor("ps_misc", [P, CHUNK], F32))
        ps_gates = ps_misc[:, 0:2 * T * M].rearrange("p (t a m) -> p t a m", t=T, a=2)
        ps_route = ps_misc[:, 2 * T * M:2 * T * M + E]
        ps_comb = ps_misc[0:M * T, P:2 * P]
        ps_vecs = ps_misc[:, 0:VECS]
        ps_bias = ps_misc[:, P:P + E]
        ps_tok = ps_aux[:].rearrange("p b (a d) -> p (b a) d", a=2)

        vecs_loaded, gw_loaded, misc_loaded = sem("vecs_loaded"), sem("gw_loaded"), sem("misc_loaded")
        w_loaded = [[sem(f"w_loaded{m}_{kind}") for kind in KINDS] for m in range(M)]
        experts_loaded = sem("experts_loaded")
        rows_zero, pool_consts = sem("rows_zero"), sem("pool_consts")
        consts, ident_zero, ident_ready = sem("consts"), sem("ident_zero"), sem("ident_ready")
        vecs_turned, vecs_ready = sem("vecs_turned"), sem("vecs_ready")
        w_hi_ready, w_lo_ready = sem("w_hi_ready"), sem("w_lo_ready")
        gw_hi_ready, gw_lo_ready = sem("gw_hi_ready"), sem("gw_lo_ready")
        bn_root_in, bn_root, prep_link = sem("bn_root_in"), sem("bn_root"), sem("prep_link")
        bias_turned, experts_ready = sem("bias_turned"), sem("experts_ready")
        main_filled = sem("main_filled")
        main_read = sem("main_read")
        decay_ready = sem("decay_ready")
        input_ready = sem("input_ready")
        scanned = sem("scanned")
        carried = sem("carried")
        weighed = sem("weighed")
        summed = sem("summed")
        x_loaded = [sem(f"x_loaded{c}") for c in range(C)]
        x_link = sem("x_link")
        x_root_in, x_root, x_scaled = sem("x_root_in"), sem("x_root"), sem("x_scaled")
        x_normed = sem("x_normed")
        x_turned = sem("x_turned")
        xh_ready, xl_ready = sem("xh_ready"), sem("xl_ready")
        gates_done, mix_link, margin_ready = sem("gates_done"), sem("mix_link"), sem("margin_ready")
        share_ready, comb_ready, comb_turned = sem("share_ready"), sem("comb_ready"), sem("comb_turned")
        comb_copied, comb_saved = sem("comb_copied"), sem("comb_saved")
        comb_loaded = [sem(f"comb_loaded{m}") for m in range(M)]
        a_turned, a_link, a_root_in, a_root = sem("a_turned"), sem("a_link"), sem("a_root_in"), sem("a_root")
        t_free, t_ready, t_link = sem("t_free"), sem("t_ready"), sem("t_link")
        t_root_in, t_root, t_scaled, u_ready, u_turned = (
            sem("t_root_in"), sem("t_root"), sem("t_scaled"), sem("u_ready"), sem("u_turned"))
        t_factor, u_first_ready = sem("t_factor"), sem("u_first_ready")
        uh_ready, ul_ready = sem("uh_ready"), sem("ul_ready")
        route_link, z_ready, route_done = sem("route_link"), sem("z_ready"), sem("route_done")
        delta_ready, sig_ready, index_ready = sem("delta_ready"), sem("sig_ready"), sem("index_ready")
        index_seen, expert_loaded = sem("index_seen"), sem("expert_loaded")
        down_done, hp_ready = sem("down_done"), sem("hp_ready")
        h_ready, hh_ready = sem("h_ready"), sem("hh_ready")
        up_in_ready, up_done = sem("up_in_ready"), sem("up_done")
        y_link, y_root_in, y_root, out_link = sem("y_link"), sem("y_root_in"), sem("y_root"), sem("out_link")
        y_scaled = sem("y_scaled")
        y_used, y_normed = sem("y_used"), sem("y_normed")
        out_ready, out_stored = sem("out_ready"), sem("out_stored")

        MIX_LINKS, ROUTE_LINKS, STAT_LINKS, OUT_LINKS = 12, 13, 4, 2

        def iterations(eng, run, last):
            def turn(j, r):
                return Batch(2 * j + r, r % 2, False)
            run(turn(0, 0), turn(0, 1), None)
            with eng.Fori(0, B // 2 - 1) as j:
                for r in (1, 2):
                    run(turn(j, r), turn(j, r + 1), turn(j, r - 1))
            last(Batch(B - 1, 1, True), turn(0, B - 2))

        def chunk(c):
            return slice(c * CHUNK, (c + 1) * CHUNK)

        def tile(t):
            return slice(t * P, (t + 1) * P)

        def chunks(c):
            return range(C) if c is None else (c,)

        def tokens(c):
            return slice(0, S) if c is None else chunk(c)

        def tiles(c):
            return range(T) if c is None else range(c * T // C, (c + 1) * T // C)

        def span(c):
            return slice(tiles(c)[0], tiles(c)[-1] + 1)

        def units(c):
            return C if c is None else 1

        def done(b, c=None):
            return C * b.n + (C if c is None else c + 1)

        def pieces(b):
            if b.cut:
                return [Piece(PLANES * c + p, p, c) for c in range(C) for p in range(PLANES)]
            return [Piece(p, p, None) for p in range(PLANES)]

        def banks(b):
            return [(pc, c, kind) for pc in pieces(b) for c in chunks(pc.c) for kind in KINDS]

        def banks_before(pc):
            return 3 * pc.q * (C if pc.c is None else 1)

        def adds_before(pc):
            return ADDS * (pc.c or 0) + max(pc.plane - KT, 0)

        y_rows = x_in[:, 0]

        def staged(buf, pc, c):
            return buf[:, pc.q % 2, tokens(c) if pc.c is None else chunk(pc.q // 2 % 2)]

        def states(pc):
            return hid[:, pc.q % 4, tokens(None) if pc.c is None else chunk(pc.q // 4 % 2)]

        def t_rows(b):
            return x_in[:, b.par] if b.cut else resid

        block = ctx.enter_context(nc.Block())

        @block.sync
        def _(sp):
            def load_x_chunk(b, c):
                sp.dma_start(x_in[:, b.par, span(c)],
                             x_t[bass.ds(b.n, 1), :, span(c)].rearrange("a p t d -> p (a t) d")
                             ).then_inc(x_loaded[c], 16)

            def load_x(b):
                for c in range(C):
                    load_x_chunk(b, c)

            def load_matrix(m, kind):
                w = {GATE: Wg, DECAY: Wd, VALUE: Wv}[kind]
                sp.dma_start(w_stage[:, m % 2, kind], w[m].rearrange("(k p) e -> p k e", p=P)
                             ).then_inc(w_loaded[m][kind], 16)

            def load_mixer(m):
                for kind in KINDS:
                    load_matrix(m, kind)

            def load_comb(nx, m):
                sp.dma_start(comb_all[:, m, :],
                             comb_dram[nx.par, m * S:(m + 1) * S].rearrange("(a s) -> a s", a=1)
                             .broadcast_to([P, S])).then_inc(comb_loaded[m], 16)

            def save_comb(nx):
                sp.wait_ge(comb_copied, nx.n + 1)
                sp.dma_start(comb_dram[nx.par].rearrange("(r p) -> r p", p=P), comb_rows[:]
                             ).then_inc(comb_saved, 16)
                sp.wait_ge(comb_saved, 16 * nx.n + 16)

            def load_expert(pv):
                sp.wait_ge(index_ready, 2 * pv.n + 2)
                sp.sem_inc(index_seen, 1)
                e = sp.value_load(index[0:1, 0:1], min_val=0, max_val=E - 1)
                sp.dma_start(expert[:].bitcast(I32),
                             experts[:].bitcast(I32)[:, bass.ds(e, 1), :].rearrange("p a c -> p (a c)")
                             ).then_inc(expert_loaded, 16)

            def store(pv):
                sp.wait_ge(out_ready, done(pv))
                sp.dma_start(out_t[bass.ds(pv.n, 1)].rearrange("a p t d -> p (a t) d"), resid[:]
                             ).then_inc(out_stored, 16)

            first = Batch(0, 0, False)
            sp.sem_inc(t_free, 1)
            load_x_chunk(first, 0)
            load_matrix(0, GATE)
            load_x_chunk(first, 1)
            load_matrix(0, DECAY)
            load_matrix(0, VALUE)
            row = 0
            for v in (bg, bv, bd):
                sp.dma_start(vec_rows[row:row + PLANES, :], v.rearrange("m (k p) -> (m k) p", p=P)
                             ).then_inc(vecs_loaded, 16)
                row += PLANES
            for v in (ln_g, ln_b, bn_g, bn_b, bn_mean, bn_var):
                sp.dma_start(vec_rows[row:row + KT, :], v.rearrange("(k p) -> k p", p=P)
                             ).then_inc(vecs_loaded, 16)
                row += KT
            for a in range(2):
                sp.dma_start(vec_rows[row:row + E, a * H:(a + 1) * H], b_down).then_inc(vecs_loaded, 16)
            sp.dma_start(gw_stage[:], gate_W.rearrange("(k p) m -> p k m", p=P)).then_inc(gw_loaded, 16)
            load_mixer(1)
            sp.dma_start(wr[:], Wr.rearrange("(k p) e -> p k e", p=P)).then_inc(misc_loaded, 16)
            sp.dma_start(br_all[:], br.rearrange("(a e) -> a e", a=1).broadcast_to([P, E])).then_inc(misc_loaded, 16)
            for k in range(KT):
                for a in range(2):
                    sp.dma_start(down_stage[:, :, k, a * H:(a + 1) * H],
                                 W_down[:, k * P:(k + 1) * P, :].rearrange("e p h -> p e h")
                                 ).then_inc(experts_loaded, 16)
            for a in range(2):
                sp.dma_start(up_stage[a * H:(a + 1) * H], W_up.rearrange("e h d -> h e d")
                             ).then_inc(experts_loaded, 16)
            for row in (64, 96):
                sp.dma_start(up_bias_stage[row:row + 1], b_up.rearrange("(a e) d -> a e d", a=1)
                             ).then_inc(experts_loaded, 16)
            for m in (2, 3):
                sp.wait_ge(w_hi_ready, 3 * (m - 1))
                sp.wait_ge(w_lo_ready, 3 * (m - 1))
                load_mixer(m)
            save_comb(first)
            for m in range(M):
                load_comb(first, m)

            def run(bt, nx, pv):
                if pv:
                    sp.wait_ge(t_ready, done(pv))
                load_x(nx)
                if pv:
                    sp.wait_ge(experts_ready, 6)
                    load_expert(pv)
                save_comb(nx)
                for m in range(M - 1):
                    sp.wait_ge(weighed, PLANES * bt.n + KT * (m + 1))
                    load_comb(nx, m)
                if pv:
                    store(pv)
                    sp.wait_ge(out_stored, 16 * pv.n + 16)
                    sp.sem_inc(t_free, 1)
                sp.wait_ge(weighed, PLANES * bt.n + PLANES)
                load_comb(nx, M - 1)

            def last(bt, pv):
                load_expert(pv)
                load_expert(bt)
                store(pv)
                for part in range(2 * C):
                    sp.wait_ge(out_ready, C * bt.n + part + 1)
                    s = slice(part * T // (2 * C), (part + 1) * T // (2 * C))
                    sp.dma_start(out_t[bt.n, :, s], t_rows(bt)[:, s]).then_inc(out_stored, 16)
                sp.wait_ge(out_stored, 16 * (B - 1 + 2 * C))

            iterations(sp, run, last)

        @block.gpsimd
        def _(pool):
            pool.memset(ident[:], 0.0).then_inc(ident_zero, 1)
            pool.wait_ge(ident_zero, 1)
            pool.affine_select(out=ident[:], in_=ident[:], compare_op=ALU.not_equal, fill=1.0, base=0,
                               pattern=[[-1, P]], channel_multiplier=1).then_inc(ident_ready, 1)
            pool.memset(neg_half[:], -0.5).then_inc(pool_consts, 1)
            pool.memset(ones[:], 1.0).then_inc(pool_consts, 1)
            for m in range(M):
                pool.memset(rank_init[:, :, m], float(M - 1 - m)).then_inc(pool_consts, 1)
            for e in range(E):
                pool.memset(order8[:, e:e + 1], float(E - e)).then_inc(pool_consts, 1)

            def power(key, ready, rooted, b, c=None):
                pool.wait_ge(ready, done(b, c))
                pool.tensor_tensor(root[key][:, span(c)], root_in[key][:, span(c)], neg_half[:, span(c)],
                                   ALU.pow).then_inc(rooted, units(c))

            pool.wait_ge(pool_consts, 2 + M + E)
            for c in range(C):
                power("x", x_root_in, x_root, Batch(0, 0, False), c)

            def bn_power():
                pool.wait_ge(bn_root_in, 1)
                pool.tensor_tensor(small[:, 1], small[:, 0], neg_half[:, 0:KT], ALU.pow).then_inc(bn_root, 1)

            def multiply(bt, pc):
                pool.wait_ge(main_read, EVAC * bt.n + banks_before(pc) + 3 * len(chunks(pc.c)))
                v = staged(value_s, pc, pc.c)
                pool.tensor_tensor(v, staged(gate_s, pc, pc.c), v, ALU.mult).then_inc(input_ready, 1)

            def add(bt, pc):
                pool.wait_ge(weighed, PLANES * bt.n + pc.q + 1)
                if pc.plane >= 2 * KT:
                    pool.wait_ge(summed, ADDS * bt.n + adds_before(pc) - KT + 1)
                a = acc[:, bt.par, pc.plane % KT, tokens(pc.c)]
                pool.tensor_tensor(a, a, states(pc), ALU.add).then_inc(summed, 1)

            def run(bt, nx, pv):
                pcs = pieces(bt)
                if pv:
                    add(pv, pieces(pv)[-1])
                for p in range(PLANES):
                    if p == 1:
                        if pv:
                            power("a", a_root_in, a_root, pv)
                        else:
                            bn_power()
                    if p == 2 and pv:
                        power("t", t_root_in, t_root, pv)
                    if p == 3:
                        power("x", x_root_in, x_root, nx)
                    multiply(bt, pcs[p])
                    if p == 6 and pv:
                        power("y", y_root_in, y_root, pv)
                    if p >= 3:
                        add(bt, pcs[p - 1])

            def last(bt, pv):
                pcs = pieces(bt)
                add(pv, pieces(pv)[-1])
                for pc in pcs[:-1]:
                    if pc.q == 2:
                        power("a", a_root_in, a_root, pv)
                    multiply(bt, pc)
                    if pc.q == 3:
                        power("t", t_root_in, t_root, pv)
                    if pc.q == 14:
                        power("a", a_root_in, a_root, bt, 0)
                    if pc.q >= 2 and pcs[pc.q - 1].plane >= KT:
                        add(bt, pcs[pc.q - 1])
                    if pc.q == 11:
                        power("y", y_root_in, y_root, pv)
                add(bt, pcs[-2])
                power("a", a_root_in, a_root, bt, 1)
                for c in range(C):
                    power("t", t_root_in, t_root, bt, c)
                for c in range(C):
                    power("y", y_root_in, y_root, bt, c)

            iterations(pool, run, last)

        @block.scalar
        def _(act):
            first = Batch(0, 0, False)

            def mixer_high(m):
                for kind in KINDS:
                    act.wait_ge(w_loaded[m][kind], 16)
                    act.activation(w_hi[:, 3 * m + kind], w_stage[:, m % 2, kind], ACT.Copy, scale=W_SCALE
                                   ).then_inc(w_hi_ready, 1)

            def high_x(nx, c=None):
                for cc in chunks(c):
                    for k in range(KT):
                        act.wait_ge(x_turned, KT * C * nx.n + KT * cc + k + 1)
                        act.activation(xh[:, nx.par, k, chunk(cc)], ps_aux[:, KT * cc + k], ACT.Copy
                                       ).then_inc(xh_ready, 1)

            def shares(nx):
                act.wait_ge(margin_ready, nx.n + 1)
                act.activation(share[:], margin[:], ACT.Sigmoid).then_inc(share_ready, 1)

            def evacuate(bt, i, bank, first):
                pc, c, kind = bank
                m, half = divmod(pc.plane, KT)
                col = BIAS[kind] + KT * m + half
                fresh = i - banks_before(pc) < 3
                behind = 3 if bt.cut and pc.q >= 2 else 1
                if fresh and not (first and pc.q < 2) and not (bt.cut and pc.q in (2, 3)):
                    if kind == GATE:
                        act.wait_ge(input_ready, PLANES * bt.n + pc.q - behind)
                    if kind == DECAY:
                        act.wait_ge(scanned, PLANES * bt.n + pc.q - behind)
                buf = {GATE: gate_s, DECAY: decay_s, VALUE: value_s}[kind]
                act.wait_ge(main_filled, EVAC * bt.n + i + 1)
                act.activation(staged(buf, pc, c), ps_main[:, i % BANKS],
                               ACT.Tanh if kind == VALUE else ACT.Sigmoid,
                               bias=vecs[:, col:col + 1], scale=Q_W).then_inc(main_read, 1)
                if kind == VALUE and c == chunks(pc.c)[-1]:
                    act.wait_ge(main_read, EVAC * bt.n + i)
                    d = staged(decay_s, pc, pc.c)
                    act.activation(d, d, ACT.Copy, bias=0.001, scale=0.998).then_inc(decay_ready, 1)

            def high_u(pv, c=None):
                for cc in chunks(c):
                    for k in range(KT):
                        act.wait_ge(u_turned, KT * C * pv.n + KT * cc + k + 1)
                        act.activation(uh[:, k, chunk(cc)], ps_aux[:, KT * cc + k], ACT.Copy,
                                       accum_out=u_sums[:, k, cc:cc + 1]).then_inc(uh_ready, 1)

            def router_sigmoids(pv):
                act.wait_ge(delta_ready, pv.n + 1)
                act.activation(r8[:, 1], r8[:, 0], ACT.Sigmoid)
                act.activation(r8[:, 2], r8[:, 0], ACT.Sigmoid, scale=-1.0).then_inc(sig_ready, 1)

            def hidden_part(pv, c):
                act.wait_ge(down_done, done(pv, c))
                act.activation(h32[H:P, chunk(c)], ps_aux[H:P, 2 + c], ACT.Identity,
                               bias=expert[H:P, HB:HB + 2].bitcast(F32), scale=Q_W * H_SCALE).then_inc(hp_ready, 1)

            def high_h(pv, c):
                act.wait_ge(h_ready, done(pv, c))
                act.activation(up_in1[0:H, chunk(c)], h32[0:H, chunk(c)], ACT.Relu).then_inc(hh_ready, 1)

            act.wait_ge(pool_consts, 2 + M + E)
            act.activation(share[:, 0, 0:1], ones[:, 0:1], ACT.Sigmoid)
            mixer_high(0)
            high_x(first, 0)
            act.wait_ge(gw_loaded, 16)
            act.activation(gw[:, :, 0], gw_stage[:], ACT.Copy, scale=W_SCALE).then_inc(gw_hi_ready, 1)
            high_x(first, 1)
            act.wait_ge(vecs_ready, 1)

            def run(bt, nx, pv):
                for i, bank in enumerate(banks(bt)):
                    if pv:
                        if i in (24, 25):
                            high_u(pv, i - 24)
                        if i == 29:
                            router_sigmoids(pv)
                        if i in (37, 38):
                            hidden_part(pv, i - 37)
                        if i in (39, 40):
                            high_h(pv, i - 39)
                    elif i == 8:
                        shares(bt)
                    elif i in (3, 9, 15):
                        mixer_high(1 + (i - 3) // 6)
                    if i in (33, 34):
                        high_x(nx, i - 33)
                    if i == 40:
                        shares(nx)
                    evacuate(bt, i, bank, pv is None)

            def scale_rows(ts):
                for t in ts:
                    act.activation(y_rows[:, t], ps_tok[:, t], ACT.Identity, bias=add_y[:, t:t + 1],
                                   scale=mul_by["y"][:, t:t + 1]).then_inc(y_normed, 1)

            def last(bt, pv):
                for i, bank in enumerate(banks(bt)):
                    if i >= EVAC - T + 1:
                        act.wait_ge(y_scaled, pv.n + 1)
                        scale_rows([i - (EVAC - T + 1)])
                    if i in (23, 24):
                        high_u(pv, i - 23)
                    if i == 27:
                        router_sigmoids(pv)
                    if i in (33, 34):
                        hidden_part(pv, i - 33)
                    if i in (34, 35):
                        high_h(pv, i - 34)
                    evacuate(bt, i, bank, False)
                scale_rows([T - 1])
                act.wait_ge(t_scaled, done(bt, 0))
                for t in tiles(0):
                    ins = act.activation(normed[:, t], t_rows(bt)[:, t], ACT.Identity, bias=shift_t[:, t:t + 1],
                                         scale=mul_by["t"][:, t:t + 1])
                ins.then_inc(u_first_ready, 1)
                for c in range(C):
                    high_u(bt, c)
                router_sigmoids(bt)
                for c in range(C):
                    hidden_part(bt, c)
                    high_h(bt, c)
                for c in range(C):
                    act.wait_ge(y_scaled, B + c)
                    scale_rows(tiles(c))

            iterations(act, run, last)

        @block.vector
        def _(dve):
            def linker(sem_, base, unit=1):
                count = [0]

                def link(ins):
                    count[0] += unit
                    ins.then_inc(sem_, unit)
                    dve.wait_ge(sem_, base + count[0])
                return link

            def chunk_linker(sem_, links, b, c):
                return linker(sem_, C * links * b.n + links * (c or 0), units(c))

            def moments_of(key, rows, link, c=None):
                for t in tiles(c):
                    ins = dve.bn_stats(out=stats[key][:, t], in_=rows(t))
                link(ins)
                even, odd = stats[key][:, span(c), 0:3], stats[key][:, span(c), 3:6]
                mom = moments[key][:, :, span(c)]
                dve.tensor_tensor(mom[:, 0], even[:, :, 1], odd[:, :, 1], ALU.add)
                dve.tensor_tensor(mom[:, 1], even[:, :, 2], odd[:, :, 2], ALU.add)
                link(dve.tensor_tensor(mom[:, 2], even[:, :, 1], odd[:, :, 1], ALU.subtract))
                link(dve.tensor_tensor(mom[:, 3], mom[:, 2], mom[:, 2], ALU.mult))
                link(dve.scalar_tensor_tensor(mom[:, 4], mom[:, 3], D / 4, mom[:, 1], ALU.mult, ALU.add))

            def low_matrix(m, kind):
                dve.wait_ge(w_hi_ready, 3 * m + kind + 1)
                dve.scalar_tensor_tensor(w_lo[:, 3 * m + kind], w_stage[:, m % 2, kind], W_SCALE,
                                         w_hi[:, 3 * m + kind], ALU.mult, ALU.subtract).then_inc(w_lo_ready, 1)

            def mixer_low(m):
                for kind in KINDS:
                    low_matrix(m, kind)

            def x_moments(nx, c=None):
                for cc in chunks(c):
                    dve.wait_ge(x_loaded[cc], 16 * nx.n + 16)
                moments_of("x", lambda t: x_in[:, nx.par, t], chunk_linker(x_link, STAT_LINKS, nx, c), c)
                dve.tensor_scalar(root_in["x"][:, span(c)], moments["x"][:, 4, span(c)], 1 / D, EPS,
                                  ALU.mult, ALU.add).then_inc(x_root_in, units(c))

            def normalise(key, rows, root_ready, scaled, ready, b, c=None):
                dve.wait_ge(root_ready, done(b, c))
                s = span(c)
                dve.tensor_scalar(mul_by[key][:, s], root[key][:, s], X_SCALE, None, ALU.mult)
                dve.tensor_scalar(mean[key][:, s], moments[key][:, 0, s], 0.5, None, ALU.mult
                                  ).then_inc(scaled, units(c))
                dve.wait_ge(scaled, done(b, c))
                for t in tiles(c):
                    ins = dve.tensor_scalar(normed[:, t], rows[:, t], mean[key][:, t:t + 1],
                                            mul_by[key][:, t:t + 1], ALU.subtract, ALU.mult)
                ins.then_inc(ready, units(c))

            def normalise_x(nx, c=None):
                normalise("x", x_in[:, nx.par], x_root, x_scaled, x_normed, nx, c)

            def normalise_t(pv, c=None):
                normalise("t", t_rows(pv), t_root, t_scaled, u_ready, pv, c)

            def scale_t(b, c):
                dve.wait_ge(t_root, done(b, c))
                s = span(c)
                dve.tensor_scalar(mul_by["t"][:, s], root["t"][:, s], X_SCALE, None, ALU.mult).then_inc(t_factor, 1)
                dve.wait_ge(t_factor, 1)
                dve.scalar_tensor_tensor(shift_t[:, s], moments["t"][:, 0, s], -0.5, mul_by["t"][:, s],
                                         ALU.mult, ALU.mult).then_inc(t_scaled, units(c))

            def low_x(nx, c=None):
                for cc in chunks(c):
                    for k in range(KT):
                        dve.wait_ge(xh_ready, KT * C * nx.n + KT * cc + k + 1)
                        dve.tensor_tensor(xl[:, nx.par, k, chunk(cc)], ps_aux[:, KT * cc + k],
                                          xh[:, nx.par, k, chunk(cc)], ALU.subtract).then_inc(xl_ready, 1)

            def rank_mixers(nx):
                link = linker(mix_link, MIX_LINKS * nx.n)
                dve.wait_ge(gates_done, nx.n + 1)
                link(dve.tensor_scalar(logit[:], ps_gates[:, :, 0], Q_W, None, ALU.mult))
                link(dve.scalar_tensor_tensor(logit[:], ps_gates[:, :, 1], Q_W, logit[:], ALU.mult, ALU.add))
                b = beats[:].rearrange("p c t -> p t c")
                pairs, at = [], 0
                for d in range(1, M):
                    n = M - d
                    ins = dve.tensor_tensor(b[:, :, at:at + n], logit[:, :, 0:n], logit[:, :, d:M], ALU.is_ge)
                    pairs.append((d, n, at))
                    at += n
                link(ins)
                src = rank_init
                for d, n, at in pairs:
                    if d == 1:
                        dve.tensor_copy(rank[:, :, M - 1:M], rank_init[:, :, M - 1:M])
                    link(dve.tensor_tensor(rank[:, :, 0:n], src[:, :, 0:n], b[:, :, at:at + n], ALU.subtract))
                    link(dve.tensor_tensor(rank[:, :, d:M], rank[:, :, d:M], b[:, :, at:at + n], ALU.add))
                    src = rank
                link(dve.tensor_scalar(chosen[:], rank[:], 1.5, None, ALU.is_lt))
                link(dve.tensor_tensor(chosen_logit[:], chosen[:], logit[:], ALU.mult))
                link(dve.tensor_reduce(pair_sum[:], chosen_logit[:], AX.X, ALU.add))
                dve.scalar_tensor_tensor(margin[:], logit[:], 2.0, pair_sum[:].broadcast_to([P, T, M]),
                                         ALU.mult, ALU.subtract).then_inc(margin_ready, 1)

            def weights_of(nx):
                dve.wait_ge(share_ready, nx.n + 1)
                dve.tensor_tensor(comb[:].rearrange("p m t -> p t m"), share[:], chosen[:], ALU.mult
                                  ).then_inc(comb_ready, 1)

            def copy_weights(nx, first):
                dve.wait_ge(comb_turned, nx.n + 1)
                if not first:
                    dve.wait_ge(comb_saved, 16 * nx.n)
                dve.tensor_copy(comb_rows[:], ps_comb).then_inc(comb_copied, 1)

            def scan(bt, pc, first):
                dve.wait_ge(decay_ready, PLANES * bt.n + pc.q + 1)
                dve.wait_ge(input_ready, PLANES * bt.n + pc.q + 1)
                if pc.q < 4:
                    if not first:
                        dve.wait_ge(summed, ADDS * bt.n + pc.q - 3)
                elif not bt.cut or pc.q >= 8:
                    user = pieces(bt)[pc.q - (8 if bt.cut else 4)]
                    if user.plane >= KT:
                        dve.wait_ge(summed, ADDS * bt.n + adds_before(user) + 1)
                start = 0.0
                if pc.c:
                    dve.wait_ge(carried, pc.plane + 1)
                    start = carry[:, pc.plane:pc.plane + 1]
                dve.tensor_tensor_scan(states(pc), staged(decay_s, pc, pc.c), staged(value_s, pc, pc.c), start,
                                       ALU.mult, ALU.add).then_inc(scanned, 1)

            def weigh(bt, pc):
                m, half = divmod(pc.plane, KT)
                dve.wait_ge(scanned, PLANES * bt.n + pc.q + 1)
                if half == 0:
                    dve.wait_ge(comb_loaded[m], 16 * bt.n + 16)
                src = states(pc)
                if pc.c == 0:
                    dve.tensor_copy(carry[:, pc.plane:pc.plane + 1], src[:, CHUNK - 1:CHUNK]).then_inc(carried, 1)
                    dve.wait_ge(carried, pc.plane + 1)
                dst = acc[:, bt.par, half, tokens(pc.c)] if m == 0 else src
                dve.tensor_tensor(dst, src, comb_all[:, m, tokens(pc.c)], ALU.mult).then_inc(weighed, 1)

            def multiply(bt, pc):
                dve.wait_ge(main_read, EVAC * bt.n + banks_before(pc) + 3)
                v = staged(value_s, pc, pc.c)
                dve.tensor_tensor(v, staged(gate_s, pc, pc.c), v, ALU.mult).then_inc(input_ready, 1)

            def add(bt, pc):
                dve.wait_ge(weighed, PLANES * bt.n + pc.q + 1)
                dve.wait_ge(summed, ADDS * bt.n + adds_before(pc))
                a = acc[:, bt.par, pc.plane % KT, tokens(pc.c)]
                dve.tensor_tensor(a, a, states(pc), ALU.add).then_inc(summed, 1)

            def a_moments(pv, c=None):
                dve.wait_ge(a_turned, done(pv, c))
                moments_of("a", lambda t: ps_tok[:, t], chunk_linker(a_link, STAT_LINKS, pv, c), c)
                dve.tensor_scalar(root_in["a"][:, span(c)], moments["a"][:, 4, span(c)], 1 / D, EPS,
                                  ALU.mult, ALU.add).then_inc(a_root_in, units(c))

            def residual(pv, c=None):
                dve.wait_ge(a_root, done(pv, c))
                if not pv.cut:
                    dve.wait_ge(t_free, pv.n + 1)
                s = span(c)
                dve.scalar_tensor_tensor(shift_a[:, s], moments["a"][:, 0, s], 0.5, root["a"][:, s],
                                         ALU.mult, ALU.mult)
                for t in tiles(c):
                    ins = dve.scalar_tensor_tensor(t_rows(pv)[:, t], ps_tok[:, t], root["a"][:, t:t + 1],
                                                   x_in[:, pv.par, t], ALU.mult, ALU.add)
                ins.then_inc(t_ready, units(c))

            def t_moments(pv, c=None):
                dve.wait_ge(t_ready, done(pv, c))
                moments_of("t", lambda t: t_rows(pv)[:, t], chunk_linker(t_link, STAT_LINKS, pv, c), c)
                dve.tensor_scalar(root_in["t"][:, span(c)], moments["t"][:, 4, span(c)], (1.0 + EPS) / D, EPS * EPS,
                                  ALU.mult, ALU.add).then_inc(t_root_in, units(c))

            def low_u(pv, c=None):
                for cc in chunks(c):
                    for k in range(KT):
                        dve.wait_ge(uh_ready, KT * C * pv.n + KT * cc + k + 1)
                        dve.tensor_tensor(ul[:, k, chunk(cc)], ps_aux[:, KT * cc + k], uh[:, k, chunk(cc)],
                                          ALU.subtract).then_inc(ul_ready, 1)

            def route_in(pv):
                link = linker(route_link, ROUTE_LINKS * pv.n)
                dve.wait_ge(uh_ready, KT * C * (pv.n + 1))
                link(dve.tensor_tensor(z_mean[:, 0], u_sums[:, :, 0], u_sums[:, :, 1], ALU.add))
                link(dve.tensor_tensor(z_mean[:, 1], z_mean[:, 0], route_mul[:], ALU.mult))
                link(dve.tensor_tensor(z_mean[:, 2], z_mean[:, 1], route_add[:], ALU.add))
                link(dve.tensor_scalar(z_wr[:, 0], wr[:, 0], z_mean[:, 2, 0:1], None, ALU.mult))
                dve.scalar_tensor_tensor(z_wr[:, 1], wr[:, 1], z_mean[:, 2, 1:2], z_wr[:, 0], ALU.mult, ALU.add
                                         ).then_inc(z_ready, 1)

            def route_logits(pv):
                link = linker(route_link, ROUTE_LINKS * pv.n + 4)
                dve.wait_ge(route_done, pv.n + 1)
                link(dve.tensor_tensor(r8[:, 3], ps_route, br_all[:], ALU.add))
                link(dve.tensor_reduce(r1[:, 0:1], r8[:, 3], AX.X, ALU.max))
                dve.tensor_scalar(r8[:, 0], r8[:, 3], r1[:, 0:1], None, ALU.subtract).then_inc(delta_ready, 1)

            def route_pick(pv):
                link = linker(route_link, ROUTE_LINKS * pv.n + 6)
                dve.wait_ge(sig_ready, pv.n + 1)
                link(dve.reciprocal(r8[:, 4], r8[:, 2]))
                link(dve.tensor_tensor(r8[:, 5], r8[:, 4], r8[:, 1], ALU.mult))
                link(dve.tensor_reduce(r1[:, 1:2], r8[:, 5], AX.X, ALU.add))
                link(dve.reciprocal(r1[:, 2:3], r1[:, 1:2]))
                link(dve.tensor_scalar(r8[:, 6], r8[:, 5], r1[:, 2:3], None, ALU.mult))
                link(dve.tensor_reduce(r1[:, 3:4], r8[:, 6], AX.X, ALU.max))
                link(dve.scalar_tensor_tensor(r8[:, 7], r8[:, 6], r1[:, 3:4], order8[:], ALU.is_equal, ALU.mult))
                dve.tensor_reduce(r1[:, 4:5], r8[:, 7], AX.X, ALU.max).then_inc(index_ready, 1)
                dve.wait_ge(index_ready, 2 * pv.n + 1)
                dve.tensor_scalar(index[:], r1[:, 4:5], -1.0, float(E), ALU.mult, ALU.add).then_inc(index_ready, 1)
                dve.tensor_scalar(r1[:, 5:6], r1[:, 3:4], 1 / (H_SCALE * W_SCALE), None, ALU.mult)

            def join_h(pv, c):
                dve.wait_ge(hp_ready, done(pv, c))
                dve.scalar_tensor_tensor(h32[0:H, chunk(c)], ps_aux[0:H, 2 + c], Q_W * H_SCALE, h32[H:P, chunk(c)],
                                         ALU.mult, ALU.add).then_inc(h_ready, 1)

            def low_h(pv, c=None):
                for cc in chunks(c):
                    dve.wait_ge(hh_ready, done(pv, cc))
                dve.tensor_copy(up_in2[0:H, tokens(c)], up_in1[0:H, tokens(c)])
                dve.scalar_tensor_tensor(up_in1[H:P, tokens(c)], h32[0:H, tokens(c)], 0.0, up_in1[0:H, tokens(c)],
                                         ALU.max, ALU.subtract).then_inc(up_in_ready, units(c))

            def y_moments(pv, c=None):
                dve.wait_ge(up_done, done(pv, c))
                if c != 1:
                    dve.scalar_tensor_tensor(r1[:, 6:7], r1[:, 5:6], 1 / D, r1[:, 5:6], ALU.mult, ALU.mult)
                moments_of("y", lambda t: ps_tok[:, t], chunk_linker(y_link, STAT_LINKS, pv, c), c)
                dve.tensor_scalar(root_in["y"][:, span(c)], moments["y"][:, 4, span(c)], r1[:, 6:7], EPS,
                                  ALU.mult, ALU.add).then_inc(y_root_in, units(c))

            def scale_y(pv, c=None):
                link = chunk_linker(out_link, OUT_LINKS, pv, c)
                s = span(c)
                dve.wait_ge(y_root, done(pv, c))
                link(dve.tensor_scalar(mul_by["y"][:, s], root["y"][:, s], r1[:, 5:6], None, ALU.mult))
                link(dve.scalar_tensor_tensor(add_y[:, s], moments["y"][:, 0, s], -0.5, mul_by["y"][:, s],
                                              ALU.mult, ALU.mult))
                dve.tensor_tensor(add_y[:, s], add_y[:, s], shift_a[:, s], ALU.subtract).then_inc(y_scaled, 1)

            def add_scaled(pv):
                for t in range(T):
                    ins = dve.scalar_tensor_tensor(resid[:, t], ps_tok[:, t], mul_by["y"][:, t:t + 1],
                                                   resid[:, t], ALU.mult, ALU.add)
                ins.then_inc(y_used, 1)

            def shift_out(pv):
                dve.wait_ge(y_used, pv.n + 1)
                dve.wait_ge(y_scaled, pv.n + 1)
                for t in range(T):
                    ins = dve.tensor_scalar(resid[:, t], resid[:, t], add_y[:, t:t + 1], None, ALU.add)
                ins.then_inc(out_ready, C)

            def finish_late(b, c):
                rows = t_rows(b)
                for t in tiles(c):
                    dve.wait_ge(y_normed, T * b.cut + t + 1)
                    ins = dve.tensor_tensor(rows[:, t], y_rows[:, t], rows[:, t], ALU.add)
                    if b.cut and t % 2:
                        ins.then_inc(out_ready, 1)
                if not b.cut:
                    ins.then_inc(out_ready, C)

            first = Batch(0, 0, False)
            dve.memset(up_in2[H:P, :], 0.0)
            dve.memset(experts[H:P, :, UP2:HB], 0.0).then_inc(rows_zero, 1)
            x_moments(first, 0)
            low_matrix(0, GATE)
            normalise_x(first, 0)
            x_moments(first, 1)
            low_x(first, 0)
            normalise_x(first, 1)
            low_matrix(0, DECAY)
            dve.wait_ge(vecs_turned, 1)
            dve.tensor_copy(vecs[:], ps_vecs).then_inc(vecs_ready, 1)
            low_matrix(0, VALUE)
            low_x(first, 1)
            dve.wait_ge(gw_hi_ready, 1)
            dve.scalar_tensor_tensor(gw[:, :, 1], gw_stage[:], W_SCALE, gw[:, :, 0], ALU.mult, ALU.subtract
                                     ).then_inc(gw_lo_ready, 1)
            dve.wait_ge(pool_consts, 2 + M + E)

            def prepare_router(link):
                dve.wait_ge(vecs_ready, 1)
                v = {k: vecs[:, c:c + KT] for k, c in (("g", LN_G), ("b", LN_B), ("bg", BN_G), ("bb", BN_B),
                                                       ("mean", BN_MEAN), ("var", BN_VAR))}
                dve.tensor_scalar(small[:, 0], v["var"], EPS, None, ALU.add).then_inc(bn_root_in, 1)
                dve.wait_ge(bn_root, 1)
                link(dve.tensor_tensor(small[:, 2], small[:, 1], v["bg"], ALU.mult))
                link(dve.tensor_tensor(small[:, 3], v["b"], v["mean"], ALU.subtract))
                link(dve.tensor_tensor(small[:, 4], small[:, 3], small[:, 2], ALU.mult))
                link(dve.tensor_tensor(route_add[:], small[:, 4], v["bb"], ALU.add))
                link(dve.scalar_tensor_tensor(route_mul[:], small[:, 2], 1 / (X_SCALE * S), v["g"], ALU.mult, ALU.mult))

            def prepare_down(link, k):
                dve.wait_ge(experts_loaded, 16 * 8)
                if k == 0:
                    link(dve.tensor_scalar(small[:, 5], vecs[:, LN_G:LN_G + KT], W_SCALE, None, ALU.mult))
                hi = experts[:, :, (2 * k) * H:(2 * k + 1) * H]
                lo = experts[:, :, (2 * k + 1) * H:(2 * k + 2) * H]
                w = down_stage[:, :, k, 0:H]
                link(dve.tensor_scalar(hi, w, small[:, 5, k:k + 1], None, ALU.mult))
                dve.scalar_tensor_tensor(lo, w, small[:, 5, k:k + 1], hi, ALU.mult, ALU.subtract
                                         ).then_inc(experts_ready, 1)

            def prepare_up(link):
                up1 = experts[:, :, UP1:UP2]
                up2 = experts[:, :, UP2:HB]
                link(dve.tensor_scalar(up1, up_stage, W_SCALE, None, ALU.mult))
                dve.scalar_tensor_tensor(up2[0:H], up_stage[0:H], W_SCALE, up1[0:H], ALU.mult, ALU.subtract
                                         ).then_inc(experts_ready, 1)

            def prepare_biases(link):
                up2 = experts[:, :, UP2:HB]
                for row in (64, 96):
                    r = slice(row, row + 1)
                    ins = dve.tensor_scalar(up2[r], up_bias_stage[r], W_SCALE, None, ALU.mult)
                    if row == 64:
                        ins.then_inc(experts_ready, 1)
                link(ins)
                dve.scalar_tensor_tensor(up2[r], up_bias_stage[r], W_SCALE, up2[r], ALU.mult, ALU.subtract
                                         ).then_inc(experts_ready, 1)
                dve.wait_ge(bias_turned, 1)
                link(dve.tensor_tensor(r8[:, 0], ps_bias, vecs[:, B_DOWN:B_DOWN + E], ALU.add))
                dve.tensor_scalar(experts[:, :, HB:HB + 2].bitcast(F32).rearrange("p e a -> p (e a)"), r8[:, 0],
                                  H_SCALE, None, ALU.mult).then_inc(experts_ready, 1)

            def piece(b, pc, first=False):
                scan(b, pc, first)
                weigh(b, pc)

            def run(bt, nx, pv):
                pcs = pieces(bt)
                if pv:
                    a_moments(pv)
                else:
                    prep = linker(prep_link, 0)
                    mixer_low(1)
                    rank_mixers(bt)
                    weights_of(bt)
                    prepare_router(prep)
                    dve.wait_ge(rows_zero, 1)
                    for row in (64, 96):
                        dve.memset(up_in2[row:row + 1, :], H_SCALE).then_inc(consts, 1)
                    copy_weights(bt, True)
                    mixer_low(2)
                piece(bt, pcs[0], pv is None)
                if pv:
                    residual(pv)
                    t_moments(pv)
                else:
                    prepare_down(prep, 0)
                    mixer_low(3)
                piece(bt, pcs[1], pv is None)
                if pv:
                    normalise_t(pv)
                piece(bt, pcs[2], pv is None)
                x_moments(nx)
                if pv:
                    route_in(pv)
                    low_u(pv)
                    dve.wait_ge(u_turned, KT * C * (pv.n + 1))
                else:
                    dve.wait_ge(x_turned, KT * C)
                normalise_x(nx)
                if pv:
                    route_logits(pv)
                piece(bt, pcs[3], pv is None)
                if pv:
                    route_pick(pv)
                low_x(nx)
                piece(bt, pcs[4])
                if pv:
                    for c in range(C):
                        join_h(pv, c)
                rank_mixers(nx)
                if pv:
                    low_h(pv)
                else:
                    prepare_down(prep, 1)
                piece(bt, pcs[5])
                weights_of(nx)
                if pv:
                    y_moments(pv)
                copy_weights(nx, False)
                if not pv:
                    prepare_up(prep)
                piece(bt, pcs[6])
                if pv:
                    scale_y(pv)
                    add_scaled(pv)
                else:
                    prepare_biases(prep)
                piece(bt, pcs[7])
                if pv:
                    shift_out(pv)

            def last(bt, pv):
                pcs = pieces(bt)
                a_moments(pv)
                piece(bt, pcs[0])
                residual(pv)
                piece(bt, pcs[1])
                t_moments(pv)
                piece(bt, pcs[2])
                normalise_t(pv)
                for q in (3, 4, 5):
                    piece(bt, pcs[q])
                route_in(pv)
                piece(bt, pcs[6])
                route_logits(pv)
                low_u(pv)
                route_pick(pv)
                piece(bt, pcs[7])
                for q in (8, 9):
                    piece(bt, pcs[q])
                for c in range(C):
                    join_h(pv, c)
                low_h(pv)
                piece(bt, pcs[10])
                y_moments(pv)
                piece(bt, pcs[11])
                scale_y(pv)
                for q in (12, 13):
                    piece(bt, pcs[q])
                a_moments(bt, 0)
                piece(bt, pcs[14])
                multiply(bt, pcs[15])
                piece(bt, pcs[15])
                add(bt, pcs[15])
                residual(bt, 0)
                a_moments(bt, 1)
                t_moments(bt, 0)
                residual(bt, 1)
                scale_t(bt, 0)
                t_moments(bt, 1)
                normalise_t(bt, 1)
                low_u(bt, 0)
                route_in(bt)
                low_u(bt, 1)
                route_logits(bt)
                route_pick(bt)
                finish_late(pv, None)
                for c in range(C):
                    join_h(bt, c)
                    low_h(bt, c)
                for c in range(C):
                    y_moments(bt, c)
                for c in range(C):
                    scale_y(bt, c)
                for c in range(C):
                    finish_late(bt, c)

            iterations(dve, run, last)

        @block.tensor
        def _(pe):
            def turn_rows(ready, c):
                for cc in chunks(c):
                    for k in range(KT):
                        for t in tiles(cc):
                            ins = pe.transpose(ps_aux[:, KT * cc + k, tile(t % (T // C))],
                                               normed[:, t, k * P:(k + 1) * P], ident[:])
                        ins.then_inc(ready, 1)

            def turn_x(nx, c=None):
                pe.wait_ge(x_normed, done(nx, c))
                turn_rows(x_turned, c)

            def gates(nx):
                pe.wait_ge(xh_ready, KT * C * (nx.n + 1))
                pe.wait_ge(xl_ready, KT * C * (nx.n + 1))
                for t in range(T):
                    n = 0
                    for k in range(KT):
                        for v in (xh, xl):
                            ins = pe.matmul(ps_gates[:, t].rearrange("p a m -> p (a m)"), v[:, nx.par, k, tile(t)],
                                            gw[:, k].rearrange("p a m -> p (a m)"),
                                            start=(n == 0), stop=(n == 2 * KT - 1))
                            n += 1
                ins.then_inc(gates_done, 1)

            def turn_weights(nx):
                pe.wait_ge(comb_ready, nx.n + 1)
                pe.transpose(ps_comb, comb[:].rearrange("p m t -> p (m t)"), ident[:]).then_inc(comb_turned, 1)

            def product(bt, i, bank, first):
                pc, c, kind = bank
                m, half = divmod(pc.plane, KT)
                if pc.plane == 0 and kind == GATE:
                    pe.wait_ge(xh_ready, KT * C * bt.n + KT * (c + 1))
                    pe.wait_ge(xl_ready, KT * C * bt.n + KT * (c + 1))
                if first and half == 0 and c == 0:
                    pe.wait_ge(w_hi_ready, 3 * m + kind + 1)
                    pe.wait_ge(w_lo_ready, 3 * m + kind + 1)
                if not (first and i < BANKS):
                    pe.wait_ge(main_read, EVAC * bt.n + i - BANKS + 1)
                n = 0
                for k in range(KT):
                    for w, v in ((w_hi, xh), (w_lo, xh), (w_hi, xl)):
                        ins = pe.matmul(ps_main[:, i % BANKS], w[:, 3 * m + kind, k, half * P:(half + 1) * P],
                                        v[:, bt.par, k, chunk(c)], start=(n == 0), stop=(n == 3 * KT - 1))
                        n += 1
                ins.then_inc(main_filled, 1)

            def turn_a(pv, c=None):
                pe.wait_ge(summed, ADDS * pv.n + ADDS * (1 + (c or 0)))
                for t in tiles(c):
                    for k in range(KT):
                        ins = pe.transpose(ps_tok[:, t, k * P:(k + 1) * P], acc[:, pv.par, k, tile(t)], ident[:])
                ins.then_inc(a_turned, units(c))

            def turn_u(pv, c=None):
                if c == 0:
                    pe.wait_ge(u_first_ready, 1)
                else:
                    pe.wait_ge(u_ready, C * pv.n + units(c))
                turn_rows(u_turned, c)

            def route(pv):
                pe.wait_ge(z_ready, pv.n + 1)
                pe.matmul(ps_route, ones[:], z_wr[:, 1], start=True, stop=True).then_inc(route_done, 1)

            def down(pv):
                pe.wait_ge(expert_loaded, 16 * pv.n + 16)
                pe.wait_ge(ul_ready, KT * C * (pv.n + 1))
                for c in range(C):
                    i = 0
                    for k in range(KT):
                        for v in (uh, ul):
                            ins = pe.matmul(ps_aux[:, 2 + c], expert[:, 2 * k * H:(2 * k + 2) * H],
                                            v[:, k, chunk(c)], start=(i == 0), stop=(i == 2 * KT - 1))
                            i += 1
                    ins.then_inc(down_done, 1)

            def up(pv, c=None):
                pe.wait_ge(up_in_ready, done(pv, c))
                for t in tiles(c):
                    pe.matmul(ps_tok[:, t], up_in1[:, tile(t)], expert[:, UP1:UP2], start=True, stop=False)
                    ins = pe.matmul(ps_tok[:, t], up_in2[:, tile(t)], expert[:, UP2:HB], start=False, stop=True)
                ins.then_inc(up_done, units(c))

            first = Batch(0, 0, False)
            pe.wait_ge(ident_ready, 1)
            turn_x(first, 0)

            def hidden_bias():
                pe.wait_ge(experts_loaded, 16 * 8)
                pe.wait_ge(misc_loaded, 32)
                pe.wait_ge(consts, 2)
                pe.wait_ge(comb_copied, 1)
                for e in range(E):
                    for k in range(KT):
                        ins = pe.matmul(ps_bias[:, e:e + 1], down_stage[:, e, k], vecs[:, LN_B + k:LN_B + k + 1],
                                        start=(k == 0), stop=(k == KT - 1))
                ins.then_inc(bias_turned, 1)

            def run(bt, nx, pv):
                for i, bank in enumerate(banks(bt)):
                    if not pv:
                        if i == 1:
                            pe.wait_ge(vecs_loaded, 16 * 11)
                            pe.transpose(ps_vecs, vec_rows[:], ident[0:VECS, 0:VECS]).then_inc(vecs_turned, 1)
                            turn_x(bt, 1)
                        if i == 4:
                            pe.wait_ge(vecs_ready, 1)
                            pe.wait_ge(gw_lo_ready, 1)
                            gates(bt)
                        if i == 10:
                            turn_weights(bt)
                        if i == 20:
                            hidden_bias()
                    if pv:
                        if i == 8:
                            turn_a(pv)
                        if i == 24:
                            turn_u(pv)
                        if i == 28:
                            route(pv)
                    if i == 32:
                        if pv:
                            pe.wait_ge(ul_ready, KT * C * (pv.n + 1))
                        turn_x(nx)
                    if i == 37 and pv:
                        pe.wait_ge(xl_ready, KT * C * (nx.n + 1))
                        down(pv)
                    if i == 38:
                        gates(nx)
                    if i == 43 and pv:
                        up(pv)
                    if i == 44:
                        turn_weights(nx)
                    product(bt, i, bank, pv is None)

            def last(bt, pv):
                for i, bank in enumerate(banks(bt)):
                    if i == 8:
                        turn_a(pv)
                    if i == 23:
                        turn_u(pv)
                    if i == 27:
                        route(pv)
                    if i == 34:
                        down(pv)
                    if i == 38:
                        up(pv)
                    if i == 46:
                        pe.wait_ge(y_normed, T // C)
                        turn_a(bt, 0)
                    product(bt, i, bank, False)
                pe.wait_ge(y_normed, T)
                turn_a(bt, 1)
                turn_u(bt, 0)
                turn_u(bt, 1)
                route(bt)
                down(bt)
                for c in range(C):
                    up(bt, c)

            iterations(pe, run, last)


_INS = ["L0_attn_x", "L0_attn_Wg", "L0_attn_bg", "L0_attn_Wv", "L0_attn_bv", "L0_attn_Wd", "L0_attn_bd",
        "L0_attn_gate_W", "L0_ffn_ln_g", "L0_ffn_ln_b", "L0_ffn_bn_g", "L0_ffn_bn_b", "L0_ffn_bn_mean",
        "L0_ffn_bn_var", "L0_ffn_Wr", "L0_ffn_br", "L0_ffn_W_down", "L0_ffn_b_down", "L0_ffn_W_up",
        "L0_ffn_b_up"]


def kernel(**inputs):
    import numpy as np
    import concourse.bacc as bacc
    from concourse.bass_utils import run_bass_kernel_spmd

    nc = bacc.Bacc("TRN2", target_bir_lowering=False, num_devices=1)
    arrays, args = {}, []
    for name in _INS:
        a = np.ascontiguousarray(inputs[name])
        arrays[f"in_{name}"] = a
        args.append(nc.dram_tensor(f"in_{name}", a.shape, mybir.dt.from_np(a.dtype), kind="ExternalInput").ap())
    shape = inputs["L0_attn_x"].shape
    args.append(nc.dram_tensor("out", shape, F32, kind="ExternalOutput").ap())
    mixer_kernel(nc, *args)
    r = run_bass_kernel_spmd(nc, [arrays], core_ids=[0])
    return r.results[0]["out"]
```
